# Optimizing a Trainium2 kernel written in Bass

```python
import numpy as np
import jax
import jax.numpy as jnp

def _softmax(x, axis=-1):
    return jax.nn.softmax(x, axis=axis)

def _gelu(x):
    return jax.nn.gelu(x, approximate=True)

def _silu(x):
    return jax.nn.silu(x)

def _sigmoid(x):
    return jax.nn.sigmoid(x)

def _layernorm(x, axis=-1, eps=1e-05):
    m = jnp.mean(x, axis=axis, keepdims=True)
    v = jnp.var(x, axis=axis, keepdims=True)
    return (x - m) / jnp.sqrt(v + eps)

def _scatter_add(tgt, idx, src, axis=0):
    return tgt.at[idx].add(src)

def _segment_sum(src, seg, n):
    return jax.ops.segment_sum(src, seg, n)
kernel_name = 'mk_vit_tower_postln_d1_tok_img256_r4_0518bb'

def setup_inputs(seed: int=0):
    np.random.seed(seed)
    _w = jnp.asarray

    def _rec_inputs():
        import jax
        import jax.numpy as jnp
        _rk = jax.random.key(seed)
        x = 7.22013e-05 + 1.00017 * jax.random.normal(jax.random.fold_in(_rk, 1), (16, 1, 1024, 64), jnp.float32)
        return x
    x = _rec_inputs()

    def _L0_tok_setup():
        import jax, jax.numpy as jnp
        import numpy as np
        T, D_IN, D_INT, D_OUT, B = (1024, 64, 64, 64, 8)
        key = jax.random.key(seed)
        ks = jax.random.split(key, 12)
        s_in = 1.0 / np.sqrt(D_IN)
        s_int = 1.0 / np.sqrt(D_INT)
        return {'x_batched': jax.random.normal(ks[0], (B, 1, T, D_IN), dtype=jnp.float32), 'd_gamma_batched': jax.random.uniform(ks[1], (T, T), dtype=jnp.float32), 'Wq': jax.random.uniform(ks[2], (D_IN, D_INT), jnp.float32, -s_in, s_in), 'bq': jax.random.uniform(ks[3], (D_INT,), jnp.float32, -s_in, s_in), 'Wk': jax.random.uniform(ks[4], (D_IN, D_INT), jnp.float32, -s_in, s_in), 'bk': jax.random.uniform(ks[5], (D_INT,), jnp.float32, -s_in, s_in), 'Wv': jax.random.uniform(ks[6], (D_IN, D_INT), jnp.float32, -s_in, s_in), 'bv': jax.random.uniform(ks[7], (D_INT,), jnp.float32, -s_in, s_in), 'Wo': jax.random.uniform(ks[8], (D_INT, D_OUT), jnp.float32, -s_int, s_int), 'bo': jax.random.uniform(ks[9], (D_OUT,), jnp.float32, -s_int, s_int), 'prelu_a': jnp.float32(0.25)}
    _L0_tok_all = _L0_tok_setup()
    _L0_tok_in = {k: v for k, v in _L0_tok_all.items() if k in ('d_gamma_batched', 'Wq', 'bq', 'Wk', 'bk', 'Wv', 'bv', 'Wo', 'bo', 'prelu_a')}
    del _L0_tok_all

    def _L0_attn_setup():
        import jax, jax.numpy as jnp
        import numpy as np
        B, S, D, H, K = (8, 256, 64, 8, 5)
        DK = D // H

        def _layernorm(x, w, b, eps=1e-12):
            m = x.mean(-1, keepdims=True)
            v = ((x - m) ** 2).mean(-1, keepdims=True)
            return w * (x - m) / jnp.sqrt(v + eps) + b

        def _forward(x, conv_w, conv_b, sqrt_beta, ln_w, ln_b, q_w, q_b, k_w, k_b, v_w, v_b, out_w, out_b, gammas):
            b, s, d = x.shape
            h = gammas.shape[0]
            dk = d // h
            xc = x.transpose(0, 2, 1)
            low = jax.lax.conv_general_dilated(xc, conv_w, window_strides=(1,), padding=[(K - 1, 0)], dimension_numbers=('NCH', 'OIH', 'NCH'))
            low = low.transpose(0, 2, 1) + conv_b
            high = x - low
            hid = _layernorm(low + sqrt_beta ** 2 * high + x, ln_w, ln_b)

            def proj(w, bb):
                return (hid @ w.T + bb).reshape(b, s, h, dk).transpose(0, 2, 1, 3)
            q, k, v = (proj(q_w, q_b), proj(k_w, k_b), proj(v_w, v_b))
            scores = jnp.einsum('bhqd,bhkd->bhqk', q, k) / jnp.sqrt(jnp.float32(dk))
            mask = jnp.tril(jnp.ones((s, s), bool))
            p_ = jax.nn.softmax(jnp.where(mask, scores, -1e+32), axis=-1) * mask
            distcum = jnp.cumsum(p_, axis=-1)
            disttotal = p_.sum(-1, keepdims=True)
            idx = jnp.arange(s)
            pos = jnp.abs(idx[:, None] - idx[None, :]).astype(jnp.float32)
            dist = jax.lax.stop_gradient(jnp.sqrt(jnp.clip((disttotal - distcum) * pos, 0.0)))
            gamma = -jax.nn.softplus(gammas)[None]
            total_effect = jnp.clip(jnp.exp(dist * gamma), 1e-05, 100000.0)
            scores = jnp.where(mask, scores * total_effect, -1e+32)
            p = jax.nn.softmax(scores, axis=-1)
            p = p.at[:, :, 0, :].set(0.0)
            out = jnp.einsum('bhqk,bhkd->bhqd', p, v)
            out = out.transpose(0, 2, 1, 3).reshape(b, s, d)
            return out @ out_w.T + out_b
        key = jax.random.key(seed)
        ks = jax.random.split(key, 8)
        s = 0.05
        return dict(x=jax.random.normal(ks[0], (B, S, D), jnp.float32), conv_w=jax.random.normal(ks[1], (D, D, K), jnp.float32) * s, conv_b=jnp.zeros((D,), jnp.float32), sqrt_beta=jax.random.normal(ks[2], (1, 1, D), jnp.float32), ln_w=jnp.ones((D,), jnp.float32), ln_b=jnp.zeros((D,), jnp.float32), q_w=jax.random.normal(ks[3], (D, D), jnp.float32) * s, q_b=jnp.zeros((D,), jnp.float32), k_w=jax.random.normal(ks[4], (D, D), jnp.float32) * s, k_b=jnp.zeros((D,), jnp.float32), v_w=jax.random.normal(ks[5], (D, D), jnp.float32) * s, v_b=jnp.zeros((D,), jnp.float32), out_w=jax.random.normal(ks[6], (D, D), jnp.float32) * s, out_b=jnp.zeros((D,), jnp.float32), gammas=jax.random.normal(ks[7], (H, 1, 1), jnp.float32) * 0.1)
    _L0_attn_all = _L0_attn_setup()
    _L0_attn_in = {k: v for k, v in _L0_attn_all.items() if k in ('conv_w', 'conv_b', 'sqrt_beta', 'ln_w', 'ln_b', 'q_w', 'q_b', 'k_w', 'k_b', 'v_w', 'v_b', 'out_w', 'out_b', 'gammas')}
    del _L0_attn_all

    def _L0_ffn_setup():
        import jax, jax.numpy as jnp
        import numpy as np
        B, K, D = (128, 16, 64)
        E = 32
        H = int(D * 0.25)
        key = jax.random.key(seed)
        ks = jax.random.split(key, 7)
        d_rs = D ** (-0.5)
        h_rs = H ** (-0.5)
        x = jax.random.normal(ks[0], (B, K, D), dtype=jnp.float32)
        router_w = jax.random.uniform(ks[1], (E, D), jnp.float32, -d_rs, d_rs)
        router_b = jax.random.uniform(ks[2], (E,), jnp.float32, -d_rs, d_rs)
        W1 = jax.random.uniform(ks[3], (E, D, H), jnp.float32, -h_rs, h_rs)
        b1 = jax.random.uniform(ks[4], (E, H), jnp.float32, -h_rs, h_rs)
        W2 = jax.random.uniform(ks[5], (E, H, D), jnp.float32, -d_rs, d_rs)
        b2 = jax.random.uniform(ks[6], (E, D), jnp.float32, -d_rs, d_rs)
        return {'x': x, 'router_w': router_w, 'router_b': router_b, 'W1': W1, 'b1': b1, 'W2': W2, 'b2': b2}
    _L0_ffn_all = _L0_ffn_setup()
    _L0_ffn_in = {k: v for k, v in _L0_ffn_all.items() if k in ('router_w', 'router_b', 'W1', 'b1', 'W2', 'b2')}
    del _L0_ffn_all
    return {'x': x, 'L0_tok_d_gamma_batched': _L0_tok_in['d_gamma_batched'], 'L0_tok_Wq': _L0_tok_in['Wq'], 'L0_tok_bq': _L0_tok_in['bq'], 'L0_tok_Wk': _L0_tok_in['Wk'], 'L0_tok_bk': _L0_tok_in['bk'], 'L0_tok_Wv': _L0_tok_in['Wv'], 'L0_tok_bv': _L0_tok_in['bv'], 'L0_tok_Wo': _L0_tok_in['Wo'], 'L0_tok_bo': _L0_tok_in['bo'], 'L0_tok_prelu_a': _L0_tok_in['prelu_a'], 'L0_attn_conv_w': _L0_attn_in['conv_w'], 'L0_attn_conv_b': _L0_attn_in['conv_b'], 'L0_attn_sqrt_beta': _L0_attn_in['sqrt_beta'], 'L0_attn_ln_w': _L0_attn_in['ln_w'], 'L0_attn_ln_b': _L0_attn_in['ln_b'], 'L0_attn_q_w': _L0_attn_in['q_w'], 'L0_attn_q_b': _L0_attn_in['q_b'], 'L0_attn_k_w': _L0_attn_in['k_w'], 'L0_attn_k_b': _L0_attn_in['k_b'], 'L0_attn_v_w': _L0_attn_in['v_w'], 'L0_attn_v_b': _L0_attn_in['v_b'], 'L0_attn_out_w': _L0_attn_in['out_w'], 'L0_attn_out_b': _L0_attn_in['out_b'], 'L0_attn_gammas': _L0_attn_in['gammas'], 'L0_ffn_router_w': _L0_ffn_in['router_w'], 'L0_ffn_router_b': _L0_ffn_in['router_b'], 'L0_ffn_W1': _L0_ffn_in['W1'], 'L0_ffn_b1': _L0_ffn_in['b1'], 'L0_ffn_W2': _L0_ffn_in['W2'], 'L0_ffn_b2': _L0_ffn_in['b2']}

def reference(x, L0_tok_d_gamma_batched, L0_tok_Wq, L0_tok_bq, L0_tok_Wk, L0_tok_bk, L0_tok_Wv, L0_tok_bv, L0_tok_Wo, L0_tok_bo, L0_tok_prelu_a, L0_attn_conv_w, L0_attn_conv_b, L0_attn_sqrt_beta, L0_attn_ln_w, L0_attn_ln_b, L0_attn_q_w, L0_attn_q_b, L0_attn_k_w, L0_attn_k_b, L0_attn_v_w, L0_attn_v_b, L0_attn_out_w, L0_attn_out_b, L0_attn_gammas, L0_ffn_router_w, L0_ffn_router_b, L0_ffn_W1, L0_ffn_b1, L0_ffn_W2, L0_ffn_b2):
    import jax
    import jax.numpy as jnp

    def _L0_tok_ref(x_batched, d_gamma_batched, Wq, bq, Wk, bk, Wv, bv, Wo, bo, prelu_a):
        import jax, jax.numpy as jnp
        import numpy as np
        T, D_IN, D_INT, D_OUT, B = (1024, 64, 64, 64, 8)
        x = x_batched.reshape(x_batched.shape[0], T, D_IN)
        q = x @ Wq + bq
        k = x @ Wk + bk
        v = x @ Wv + bv
        scores = jnp.einsum('btd,bsd->bts', q, k)
        retained = jnp.einsum('bts,bsd->btd', d_gamma_batched * scores, v)
        y = retained @ Wo + bo
        out = jnp.where(y >= 0, y, prelu_a * y)
        return out

    def _L0_attn_ref(x, conv_w, conv_b, sqrt_beta, ln_w, ln_b, q_w, q_b, k_w, k_b, v_w, v_b, out_w, out_b, gammas):
        import jax, jax.numpy as jnp
        import numpy as np
        B, S, D, H, K = (8, 256, 64, 8, 5)
        DK = D // H

        def _layernorm(x, w, b, eps=1e-12):
            m = x.mean(-1, keepdims=True)
            v = ((x - m) ** 2).mean(-1, keepdims=True)
            return w * (x - m) / jnp.sqrt(v + eps) + b

        def _forward(x, conv_w, conv_b, sqrt_beta, ln_w, ln_b, q_w, q_b, k_w, k_b, v_w, v_b, out_w, out_b, gammas):
            b, s, d = x.shape
            h = gammas.shape[0]
            dk = d // h
            xc = x.transpose(0, 2, 1)
            low = jax.lax.conv_general_dilated(xc, conv_w, window_strides=(1,), padding=[(K - 1, 0)], dimension_numbers=('NCH', 'OIH', 'NCH'))
            low = low.transpose(0, 2, 1) + conv_b
            high = x - low
            hid = _layernorm(low + sqrt_beta ** 2 * high + x, ln_w, ln_b)

            def proj(w, bb):
                return (hid @ w.T + bb).reshape(b, s, h, dk).transpose(0, 2, 1, 3)
            q, k, v = (proj(q_w, q_b), proj(k_w, k_b), proj(v_w, v_b))
            scores = jnp.einsum('bhqd,bhkd->bhqk', q, k) / jnp.sqrt(jnp.float32(dk))
            mask = jnp.tril(jnp.ones((s, s), bool))
            p_ = jax.nn.softmax(jnp.where(mask, scores, -1e+32), axis=-1) * mask
            distcum = jnp.cumsum(p_, axis=-1)
            disttotal = p_.sum(-1, keepdims=True)
            idx = jnp.arange(s)
            pos = jnp.abs(idx[:, None] - idx[None, :]).astype(jnp.float32)
            dist = jax.lax.stop_gradient(jnp.sqrt(jnp.clip((disttotal - distcum) * pos, 0.0)))
            gamma = -jax.nn.softplus(gammas)[None]
            total_effect = jnp.clip(jnp.exp(dist * gamma), 1e-05, 100000.0)
            scores = jnp.where(mask, scores * total_effect, -1e+32)
            p = jax.nn.softmax(scores, axis=-1)
            p = p.at[:, :, 0, :].set(0.0)
            out = jnp.einsum('bhqk,bhkd->bhqd', p, v)
            out = out.transpose(0, 2, 1, 3).reshape(b, s, d)
            return out @ out_w.T + out_b
        return _forward(x, conv_w, conv_b, sqrt_beta, ln_w, ln_b, q_w, q_b, k_w, k_b, v_w, v_b, out_w, out_b, gammas)

    def _L0_ffn_ref(x, router_w, router_b, W1, b1, W2, b2):
        import jax, jax.numpy as jnp
        import numpy as np
        B, K, D = (128, 16, 64)
        E = 32
        H = int(D * 0.25)
        xf = x.reshape(-1, D)
        logits = xf @ router_w.T + router_b
        idx = jnp.argmax(logits, axis=-1)
        w1t = jnp.take(W1, idx, axis=0)
        h = jnp.einsum('nd,ndh->nh', xf, w1t) + jnp.take(b1, idx, axis=0)
        h = jax.nn.relu(h)
        w2t = jnp.take(W2, idx, axis=0)
        out = jnp.einsum('nh,nhd->nd', h, w2t) + jnp.take(b2, idx, axis=0)
        out = jax.nn.relu(out)
        return out.reshape(x.shape)
    h = _L0_tok_ref(x, L0_tok_d_gamma_batched, L0_tok_Wq, L0_tok_bq, L0_tok_Wk, L0_tok_bk, L0_tok_Wv, L0_tok_bv, L0_tok_Wo, L0_tok_bo, L0_tok_prelu_a)
    h = _layernorm(h + _L0_attn_ref(h, L0_attn_conv_w, L0_attn_conv_b, L0_attn_sqrt_beta, L0_attn_ln_w, L0_attn_ln_b, L0_attn_q_w, L0_attn_q_b, L0_attn_k_w, L0_attn_k_b, L0_attn_v_w, L0_attn_v_b, L0_attn_out_w, L0_attn_out_b, L0_attn_gammas), axis=-1)
    h = _layernorm(h + _L0_ffn_ref(h, L0_ffn_router_w, L0_ffn_router_b, L0_ffn_W1, L0_ffn_b1, L0_ffn_W2, L0_ffn_b2), axis=-1)
    return h

_drawn_inputs = setup_inputs


def setup_inputs(seed=0):
    import zlib

    import numpy as np

    out = dict(_drawn_inputs(seed))
    spreads = {'L0_attn_conv_b': (0.0, 2.0),
     'L0_attn_ln_w': (1.0, 0.6),
     'L0_attn_ln_b': (0.0, 0.8),
     'L0_attn_q_b': (0.0, 0.8),
     'L0_attn_k_b': (0.0, 2.0),
     'L0_attn_v_b': (0.0, 0.8),
     'L0_attn_out_b': (0.0, 0.8)}
    factors = {'L0_tok_bo': 8.0,
     'L0_attn_conv_w': 8.0,
     'L0_attn_sqrt_beta': 8.0,
     'L0_attn_q_w': 8.0,
     'L0_attn_k_w': 8.0,
     'L0_attn_v_w': 8.0,
     'L0_attn_out_w': 7.558,
     'L0_attn_gammas': 8.0,
     'L0_ffn_b1': 3.134}
    for name, (base, spread) in spreads.items():
        noise = np.random.default_rng([zlib.crc32(name.encode()), seed]).standard_normal(out[name].shape)
        drawn = base * np.exp(spread * noise) if base else spread * noise
        out[name] = jnp.asarray(drawn.astype(out[name].dtype))
    for name, factor in factors.items():
        out[name] = (out[name] * factor).astype(out[name].dtype)
    return out
```

```python
import math
from contextlib import ExitStack

import concourse.bass as bass
from concourse import mybir

ALU = mybir.AluOpType
ACT = mybir.ActivationFunctionType
AX = mybir.AxisListType
F32 = mybir.dt.float32
BF16 = mybir.dt.bfloat16
DS = bass.ds

P = 128
B, T, D = 16, 1024, 64
NB = T // P
H, DK = 8, 8
TAPS = 5
E, HID = 32, 16
KP = 96
NPART = 3
VW = DK + 1

G = 2
HP = H // G
NSTEP = B * HP
ORDER = (7, 0, 6, 1, 5, 2, 4, 3)
UNITS = [(g, qb) for g in range(G) for qb in ORDER]
NU = len(UNITS)
HEADW = sum(P * (qb + 1) for qb in range(NB))
OFF = [P * qb * (qb + 1) // 2 for qb in range(NB)]
LAG = 2
GROUPS = [(u, j, min(4, qb + 1 - j)) for u, (g, qb) in enumerate(UNITS) for j in range(0, qb + 1, 4)]
NG = len(GROUPS)
NQ = NU // 4
MASKED = -1e32
LN_FLOOR = math.log(1e-5)


def alone(eng, sem):
    eng.sem_inc(sem("passed"), 1)


def setup_phase(nc, a, st, hold):
    ident, identb, maskb, pos, gam = hold["ident"], hold["identb"], hold["maskb"], hold["pos"], hold["gam"]
    with ExitStack() as c:
        sb = lambda n, s, d=F32: c.enter_context(nc.sbuf_tensor(n, s, d))
        sem = lambda n: c.enter_context(nc.semaphore(n))
        maskf = sb("maskf", [P, P])
        e = sb("gam_exp", [P, 4, H])
        par = sb("par", [P, H, 2])
        loaded, ab, ex, ln, sp, stored, rc = (sem("set_" + n) for n in
                                              ("loaded", "abs", "exp", "ln", "sp", "stored", "rc"))
        conv = sem("set_conv")
        with nc.Block() as block:
            @block.sync
            def _(sp_):
                sp_.dma_start(ident[:], a["c_ident"]).then_inc(loaded, 16)
                sp_.dma_start(maskf[:], a["c_mask"]).then_inc(loaded, 16)
                sp_.dma_start(pos[:], a["c_pos"]).then_inc(loaded, 16)
                sp_.dma_start(gam[:], a["gammas"]).then_inc(loaded, 16)
                sp_.wait_ge(sp, 4)
                with sp_.Fori(0, B) as b:
                    for s in range(HP):
                        sp_.dma_start(st["par"][DS(b * HP + s, 1)].rearrange("a p g k -> (a p) g k"),
                                      par[:, s * G:(s + 1) * G, :]).then_inc(stored, 16)
                sp_.wait_ge(stored, 16 * NSTEP)

            @block.vector
            def _(dve):
                dve.wait_ge(loaded, 64)
                dve.tensor_copy(identb[:], ident[:]).then_inc(conv, 1)
                dve.tensor_copy(maskb[:], maskf[:]).then_inc(conv, 1)
                dve.scalar_tensor_tensor(e[:, 0], gam[:], -1.0, gam[:], ALU.mult, ALU.max).then_inc(ab, 1)
                dve.wait_ge(ln, 1)
                dve.scalar_tensor_tensor(e[:, 3], gam[:], 0.0, e[:, 2], ALU.max, ALU.add).then_inc(sp, 1)
                dve.wait_ge(sp, 1)
                dve.tensor_scalar(par[:, :, 0], e[:, 3], -1.0, None, ALU.mult).then_inc(sp, 1)
                dve.reciprocal(e[:, 0], e[:, 3]).then_inc(sp, 1)
                dve.wait_ge(sp, 3)
                dve.scalar_tensor_tensor(par[:, :, 1], e[:, 0], LN_FLOOR ** 2, e[:, 0], ALU.mult, ALU.mult).then_inc(sp, 1)

            @block.scalar
            def _(act):
                act.wait_ge(ab, 1)
                act.activation(e[:, 1], e[:, 0], ACT.Exp, scale=-1.0).then_inc(ex, 1)
                act.wait_ge(ex, 1)
                act.activation(e[:, 2], e[:, 1], ACT.Ln, bias=1.0).then_inc(ln, 1)


def token_phase(nc, a, st, hold):
    ident = hold["ident"]
    with ExitStack() as c:
        sb = lambda n, s, d=F32: c.enter_context(nc.sbuf_tensor(n, s, d))
        names = {}

        def sem(n):
            if n not in names:
                names[n] = c.enter_context(nc.semaphore("a_" + n))
            return names[n]

        gammaT = sb("gammaT", [P, NB, T])
        xT = sb("xT", [KP, T])
        wq, wk, wv = sb("wq", [KP, D]), sb("wk", [KP, D]), sb("wv", [KP, D])
        wo2 = sb("wo2", [P, D])
        bo_row, cb_row, ones_row = sb("bo_row", [KP, NB * D]), sb("cb_row", [KP, NB * D]), sb("ones_row", [KP, P])
        beta = sb("beta", [P, D])
        beta2 = sb("beta2", [P, 2, D])
        cw = sb("cw", [P, 3, D])
        prelu = sb("prelu", [P, 1])
        eps = sb("eps", [P, 1])
        ln_wb = sb("ln_wb", [D, 2])
        wqk = sb("wqk", [KP, 2 * D])
        wva = sb("wva", [KP, H * VW])
        qk_scale = sb("qk_scale", [P, 1])
        qT, kT = sb("qT", [KP, T]), sb("kT", [KP, T])
        v = sb("v", [P, NB, D])
        gm = sb("gm", [P, 2, T])
        retT = sb("retT", [P, T])
        neg = sb("neg", [P, NB, D])
        h1 = sb("h1", [P, NB, 2, D])
        hT = sb("hT", [P, T + 4])
        stat = sb("stat", [P, 4, NB])
        xc, sq = sb("xc", [P, NB, D]), sb("sq", [P, NB, D])
        nT = sb("nT", [KP, T])
        qk = sb("qk", [P, T])
        rest = sb("rest", [P, T])
        part = sb("part", [P, NPART, T], BF16)
        va = sb("va", [P, NB, H * VW])
        p0, p1, p2, p3 = (c.enter_context(nc.psum_tensor(f"pa{i}", [P, T], F32)) for i in range(4))
        half = lambda t, i: t[:, i * 512:(i + 1) * 512]
        blk = lambda t, i, w=P: t[:, i * w:(i + 1) * w]

        with nc.Block() as block:
            @block.sync
            def _(sp):
                for t, n in ((gammaT, "gammaT"), (wq, "wq"), (wk, "wk"), (wv, "wv"), (wo2, "wo2"), (bo_row, "bo_row"),
                             (cb_row, "cb_row"), (ones_row, "c_ones_row"), (beta, "beta"), (cw, "conv_w"),
                             (prelu, "prelu"), (eps, "c_eps12"), (ln_wb, "ln_wb"), (wqk, "wqk"), (wva, "wva"),
                             (qk_scale, "c_qk_scale")):
                    sp.dma_start(t[:], a[n]).then_inc(sem("weights"), 16)
                sp.sem_inc(sem("h1_stored"), 1)
                sp.sem_inc(sem("qk_stored"), 1)
                sp.sem_inc(sem("v_stored"), 1)
                with sp.Fori(0, B) as b:
                    sp.wait_ge(sem("v_proj"), b + 1)
                    sp.dma_start(xT[0:D, :], a["xT"][DS(b, 1)].rearrange("a d t -> (a d) t")).then_inc(sem("x_loaded"), 16)
                    sp.wait_ge(sem("h1"), b + 1)
                    sp.dma_start(st["h1"][DS(b, 1)].rearrange("a p n d -> (a p) n d"), h1[:, :, 0, :]).then_inc(sem("h1_stored"), 16)
                    sp.wait_ge(sem("va"), b + 1 + 1)
                    for s in range(HP):
                        sp.dma_start(st["v"][DS(b * HP + s, 1)].rearrange("a p n w -> (a p) n w"),
                                     va[:, :, s * G * VW:(s + 1) * G * VW]).then_inc(sem("v_stored"), 16)
                    sp.wait_ge(sem("part2"), b + 1)
                    for r in range(NPART):
                        for w in range(2):
                            sp.dma_start(st["qk"][DS(b * D, D), w, r], part[w * D:(w + 1) * D, r, :]).then_inc(sem("qk_stored"), 16)
                sp.wait_ge(sem("h1_stored"), 16 * B + 1)
                sp.wait_ge(sem("v_stored"), 16 * HP * B + 1)
                sp.wait_ge(sem("qk_stored"), 16 * 2 * NPART * B + 1)

            @block.gpsimd
            def _(pool):
                with pool.Fori(0, B) as b:
                    pool.wait_ge(sem("h1"), b + 1)
                    alone(pool, sem)
                    pool.tensor_copy(h1[:, :, 1, :], h1[:, :, 0, :]).then_inc(sem("h1_twice"), 1)
                    pool.wait_ge(sem("part0"), b + 1 + 1)
                    pool.tensor_tensor(rest[:], qk[:], part[:, 0, :], ALU.subtract).then_inc(sem("rest"), 1)

            @block.vector
            def _(dve):
                for t in (xT, nT, qT, kT):
                    dve.memset(t[D:KP, :], 0.0).then_inc(sem("pads"), 1)
                dve.memset(hT[:], 0.0).then_inc(sem("pads"), 1)
                dve.wait_ge(sem("pads"), 5)
                dve.memset(xT[D:D + 1, :], 1.0).then_inc(sem("pads"), 1)
                dve.memset(nT[D:D + 1, :], 1.0).then_inc(sem("pads"), 1)
                dve.wait_ge(sem("weights"), 16 * 16)
                dve.tensor_tensor(beta2[:, 0, :], beta[:], beta[:], ALU.mult).then_inc(sem("cw"), 1)
                dve.wait_ge(sem("cw"), 1)
                dve.tensor_scalar(beta2[:, 1, :], beta2[:, 0, :], 1.0, None, ALU.add).then_inc(sem("cw"), 1)
                dve.wait_ge(sem("cw"), 2)
                dve.tensor_scalar(beta2[:, 0, :], beta2[:, 0, :], -1.0, 1.0, ALU.mult, ALU.add).then_inc(sem("cw"), 1)
                dve.wait_ge(sem("cw"), 3)
                dve.tensor_tensor(cw[:], cw[:], beta2[:, 0:1, :].to_broadcast([P, 3, D]), ALU.mult).then_inc(sem("cw"), 1)
                dve.tensor_tensor(beta[0:D, :], ident[0:D, 0:D], beta2[0:D, 1, :], ALU.mult).then_inc(sem("cw"), 1)
                dve.wait_ge(sem("cw"), 5)
                dve.tensor_tensor(cw[0:D, 2, :], cw[0:D, 2, :], beta[0:D, :], ALU.add).then_inc(sem("cw"), 1)
                dve.tensor_tensor(cb_row[:].rearrange("p (n d) -> p n d", d=D), cb_row[:].rearrange("p (n d) -> p n d", d=D),
                                  beta2[0:KP, 0:1, :].to_broadcast([KP, NB, D]), ALU.mult).then_inc(sem("cw"), 1)
                dve.wait_ge(sem("pads"), 7)
                with dve.Fori(0, B) as b:
                    dve.wait_ge(sem("qk_proj"), 2 * b + 2)
                    dve.tensor_copy(kT[0:D, :], p1[0:D, :]).then_inc(sem("kT"), 1)
                    for s in range(NB):
                        dve.wait_ge(sem("scores"), NB * b + s + 1)
                        if s >= 2:
                            dve.wait_ge(sem("ret"), NB * b + s - 1)
                        dve.tensor_tensor(gm[:, s % 2, :], (p0, p1)[s % 2][:], gammaT[:, s, :], ALU.mult).then_inc(sem("gated"), 1)
                    dve.wait_ge(sem("y"), b + 1)
                    y = p2[:, 512:1024].rearrange("p (n d) -> p n d", d=D)
                    dve.tensor_scalar(neg[:], y, 0.0, prelu[:, 0:1], ALU.min, ALU.mult).then_inc(sem("neg"), 1)
                    dve.wait_ge(sem("neg"), b + 1)
                    dve.wait_ge(sem("h1_stored"), 16 * b + 1)
                    dve.scalar_tensor_tensor(h1[:, :, 0, :], y, 0.0, neg[:], ALU.max, ALU.add).then_inc(sem("h1"), 1)
                    dve.wait_ge(sem("h1T"), b + 1)
                    dve.tensor_copy(hT[D:P, 3:3 + T], p0[D:P, :]).then_inc(sem("hT_high"), 1)
                    dve.wait_ge(sem("z"), b + 1)
                    z = p1[:, 0:512].rearrange("p (n d) -> p n d", d=D)
                    dve.tensor_reduce(stat[:, 0, :], z, AX.X, ALU.add).then_inc(sem("ln"), 1)
                    dve.wait_ge(sem("ln"), 6 * b + 1)
                    dve.tensor_scalar(stat[:, 1, :], stat[:, 0, :], -1.0 / D, None, ALU.mult).then_inc(sem("ln"), 1)
                    dve.wait_ge(sem("ln"), 6 * b + 2)
                    dve.tensor_tensor(xc[:], z, stat[:, 1, :].unsqueeze(2).to_broadcast([P, NB, D]), ALU.add).then_inc(sem("ln"), 1)
                    dve.wait_ge(sem("ln"), 6 * b + 3)
                    dve.tensor_tensor(sq[:], xc[:], xc[:], ALU.mult).then_inc(sem("ln"), 1)
                    dve.wait_ge(sem("ln"), 6 * b + 4)
                    dve.tensor_reduce(stat[:, 2, :], sq[:], AX.X, ALU.add).then_inc(sem("var"), 1)
                    dve.wait_ge(sem("std"), b + 1)
                    dve.reciprocal(stat[:, 1, :], stat[:, 3, :]).then_inc(sem("ln"), 1)
                    dve.wait_ge(sem("ln"), 6 * b + 5)
                    dve.tensor_tensor(xc[:], xc[:], stat[:, 1, :].unsqueeze(2).to_broadcast([P, NB, D]), ALU.mult).then_inc(sem("ln"), 1)
                    dve.wait_ge(sem("rest"), b + 1)
                    dve.tensor_copy(part[:, 1, :], rest[:]).then_inc(sem("part1"), 1)
                    dve.wait_ge(sem("part1"), b + 1)
                    dve.tensor_tensor(part[:, 2, :], rest[:], part[:, 1, :], ALU.subtract).then_inc(sem("part2"), 1)

            @block.scalar
            def _(act):
                act.sem_inc(sem("part0"), 1)
                act.sem_inc(sem("va"), 1)
                act.wait_ge(sem("weights"), 16 * 16)
                act.wait_ge(sem("pads"), 7)
                with act.Fori(0, B) as b:
                    act.wait_ge(sem("qk_proj"), 2 * b + 1)
                    act.copy(qT[0:D, :], p0[0:D, :]).then_inc(sem("qT"), 1)
                    act.wait_ge(sem("v_proj"), b + 1 + 1)
                    act.copy(v[:].rearrange("p n d -> p (n d)"), p2[:, 0:512]).then_inc(sem("v"), 1)
                    act.wait_ge(sem("ret"), NB * b + NB)
                    act.copy(retT[:], p3[:]).then_inc(sem("retT"), 1)
                    act.wait_ge(sem("h1T"), b + 1)
                    act.copy(hT[0:D, 4:4 + T], p0[0:D, :]).then_inc(sem("hT_low"), 1)
                    act.wait_ge(sem("var"), b + 1)
                    act.activation(stat[:, 3, :], stat[:, 2, :], ACT.Sqrt, scale=1.0 / D, bias=eps[:, 0:1]).then_inc(sem("std"), 1)
                    act.wait_ge(sem("nT_ps"), b + 1)
                    act.activation(nT[0:D, :], p2[0:D, :], ACT.Identity, scale=ln_wb[:, 0:1], bias=ln_wb[:, 1:2]).then_inc(sem("nT"), 1)
                    act.wait_ge(sem("qk2"), b + 1)
                    act.wait_ge(sem("qk_stored"), 16 * 2 * NPART * b + 1)
                    act.activation(part[:, 0, :], p0[:], ACT.Copy, scale=qk_scale[:, 0:1]).then_inc(sem("part0_"), 1)
                    act.activation(qk[:], p0[:], ACT.Copy, scale=qk_scale[:, 0:1]).then_inc(sem("part0"), 1)
                    act.wait_ge(sem("va_ps"), b + 1)
                    act.wait_ge(sem("v_stored"), 16 * HP * b + 1)
                    act.copy(va[:], p1[:].rearrange("p (n w) -> p n w", w=P)[:, :, 0:H * VW]).then_inc(sem("va"), 1)

            @block.tensor
            def _(pe):
                mm = pe.matmul
                pe.sem_inc(sem("v_proj"), 1)
                pe.wait_ge(sem("weights"), 16 * 16)
                pe.wait_ge(sem("pads"), 7)
                pe.wait_ge(sem("cw"), 7)
                with pe.Fori(0, B) as b:
                    pe.wait_ge(sem("x_loaded"), 16 * b + 16)
                    pe.wait_ge(sem("part0"), b + 1)
                    pe.wait_ge(sem("va"), b + 1)
                    for w, p in ((wq, p0), (wk, p1)):
                        for n in range(2):
                            last = mm(half(p, n)[0:D, :], w[:], half(xT, n), start=True, stop=True)
                        last.then_inc(sem("qk_proj"), 1)
                    for n in range(NB):
                        last = mm(blk(p2, n, D), blk(xT, n), wv[:], start=True, stop=True)
                    last.then_inc(sem("v_proj"), 1)
                    pe.wait_ge(sem("qT"), b + 1)
                    pe.wait_ge(sem("kT"), b + 1)
                    for s in range(NB + 1):
                        if s < NB:
                            if s >= 2:
                                pe.wait_ge(sem("gated"), NB * b + s - 1)
                            for n in range(2):
                                last = mm(half((p0, p1)[s % 2], n), blk(kT, s), half(qT, n), start=True, stop=True)
                            last.then_inc(sem("scores"), 1)
                        if s >= 1:
                            t = s - 1
                            if t == 0:
                                pe.wait_ge(sem("v"), b + 1)
                            pe.wait_ge(sem("gated"), NB * b + t + 1)
                            r = D * (t % 2)
                            for n in range(2):
                                last = mm(half(p3, n)[r:r + D, :], v[:, t, :], gm[:, t % 2, n * 512:(n + 1) * 512],
                                          start=t < 2, stop=t >= NB - 2)
                            last.then_inc(sem("ret"), 1)
                    pe.wait_ge(sem("retT"), b + 1)
                    mm(p2[:, 512:1024], ones_row[:], bo_row[:], start=True, stop=False)
                    for n in range(NB):
                        last = mm(p2[:, 512 + n * D:512 + (n + 1) * D], blk(retT, n), wo2[:], start=False, stop=n == NB - 1)
                    last.then_inc(sem("y"), 1)
                    pe.wait_ge(sem("h1_twice"), b + 1)
                    for n in range(NB):
                        last = pe.transpose(blk(p0, n), h1[:, n].rearrange("p a d -> p (a d)"), ident[:])
                    last.then_inc(sem("h1T"), 1)
                    pe.wait_ge(sem("hT_low"), b + 1)
                    pe.wait_ge(sem("hT_high"), b + 1)
                    mm(p1[:, 0:512], ones_row[:], cb_row[:], start=True, stop=False)
                    for n in range(NB):
                        for k in range(3):
                            last = mm(p1[:, n * D:(n + 1) * D], hT[:, n * P + 2 * k:n * P + 2 * k + P], cw[:, k, :],
                                      start=False, stop=n == NB - 1 and k == 2)
                    last.then_inc(sem("z"), 1)
                    pe.wait_ge(sem("ln"), 6 * b + 6)
                    alone(pe, sem)
                    for n in range(NB):
                        last = pe.transpose(blk(p2, n)[0:D, :], xc[:, n, :], ident[:])
                    last.then_inc(sem("nT_ps"), 1)
                    pe.wait_ge(sem("nT"), b + 1)
                    for n in range(2):
                        last = mm(half(p0, n), wqk[:], half(nT, n), start=True, stop=True)
                    last.then_inc(sem("qk2"), 1)
                    for n in range(NB):
                        last = mm(p1[:, n * P:n * P + H * VW], blk(nT, n), wva[:], start=True, stop=True)
                    last.then_inc(sem("va_ps"), 1)


def attention_phase(nc, a, st, hold):
    ident, identb, maskb, pos = hold["ident"], hold["identb"], hold["maskb"], hold["pos"]
    with ExitStack() as c:
        sb = lambda n, s, d=F32: c.enter_context(nc.sbuf_tensor(n, s, d))
        names = {}

        def sem(n):
            if n not in names:
                names[n] = c.enter_context(nc.semaphore("b_" + n))
            return names[n]

        qs = [[sb(f"qs{p}{g}", [KP, T], BF16) for g in range(G)] for p in range(2)]
        ks = [[sb(f"ks{p}{g}", [KP, T], BF16) for g in range(G)] for p in range(2)]
        xe = [sb(f"xe{p}", [P, G, HEADW]) for p in range(2)]
        vals = [sb(f"vals{p}", [P, NB, G * VW]) for p in range(2)]
        par = [sb(f"par{p}", [P, G, 2]) for p in range(2)]
        NSC = 3
        behind = sb("behind", [P, NSC, T // 2 + 1])
        negmax = sb("negmax", [P, 2, NU])
        rtot = sb("rtot", [P, 2, NU])
        max2 = sb("max2", [P, 2, NU])
        pt = [sb(f"pt{i}", [P, 512]) for i in range(2)]
        ot = [sb(f"ot{i}", [P, 512]) for i in range(2)]
        o = sb("o", [P, G, NB, VW])
        s1 = [c.enter_context(nc.psum_tensor(f"s1_{i}", [P, T], F32)) for i in range(2)]
        s2 = c.enter_context(nc.psum_tensor("s2", [P, T], F32))
        tp = c.enter_context(nc.psum_tensor("tp", [P, 512], F32))
        op = c.enter_context(nc.psum_tensor("op", [P, 512], F32))

        POOL_ODD = lambda u: u % 2 == 0
        NODD = sum(not POOL_ODD(u) for u in range(NU))
        width = lambda u: P * (UNITS[u][1] + 1)

        def span(p, u, k0=0, k1=None):
            g, qb = UNITS[u]
            return xe[p][:, g, OFF[qb] + k0:OFF[qb] + (width(u) if k1 is None else k1)]

        def plane(p, u, odd):
            g, qb = UNITS[u]
            return xe[p][:, g, OFF[qb] + odd:OFF[qb] + width(u):2]

        def tail(u, shift):
            h = width(u) // 2
            return behind[:, u % NSC, T // 2 - h + shift:T // 2 + shift]

        def scores(pe, dst, p, u):
            g, qb = UNITS[u]
            w = width(u)
            q = qs[p][g][:, qb * P:(qb + 1) * P]
            for lo in range(0, w, 512):
                hi = min(lo + 512, w)
                pe.matmul(dst[:, lo:hi], q, ks[p][g][:, lo:hi], start=True, stop=hi < w)
            return pe.matmul(dst[:, w - P:w], identb[:], maskb[:], start=False, stop=True)

        def pe_front(pe, m, p, u, turn):
            g, qb = UNITS[u]
            if u % NB == 0:
                pe.wait_ge(sem(f"qk_loaded{g}{p}"), 32 * NPART * turn + 32 * NPART)
            if u >= 2 or not isinstance(m, int) or m > 0:
                pe.wait_ge(sem("exp1"), NU * m + u - 1)
            scores(pe, s1[u % 2], p, u).then_inc(sem("scores1"), 1)

        def pe_back_scores(pe, m, p, u):
            pe.wait_ge(sem("weighted"), NU * m + u + 1)
            scores(pe, s2, p, u).then_inc(sem("scores2"), 1)

        def pe_values(pe, m, p, k, turn):
            u, j0, n = GROUPS[k]
            g, qb = UNITS[u]
            pe.wait_ge(sem("exp2"), NG * m + k + 1)
            if k == 0:
                pe.wait_ge(sem(f"v_loaded{p}"), 32 * turn + 32)
            if j0 == 0 and u % 4 == 0:
                pe.wait_ge(sem("ot"), NQ * m + u // 4 + 1)
            for i in range(n):
                j = j0 + i
                last = pe.matmul(op[32 * i:32 * i + VW, (u % 4) * P:(u % 4 + 1) * P],
                                 vals[p][:, j, g * VW:(g + 1) * VW], pt[k % 2][:, i * P:(i + 1) * P],
                                 start=j0 == 0, stop=j + 4 > qb)
            last.then_inc(sem("products"), 1)

        def pe_back_products(pe, m, p, u, turn):
            for k, (gu, j0, n) in enumerate(GROUPS):
                if gu != u:
                    continue
                if j0 == 0:
                    pe.wait_ge(sem("shifted"), NU * m + u + 1)
                if k >= 1:
                    pe.wait_ge(sem("exp2"), NG * m + k)
                if j0 == 0 and (u == 0 or u % 4 == 2 and u > 4):
                    pe.wait_ge(sem("o"), NU * m + 4 * (u // 4) + 1)
                for i in range(n):
                    last = pe.transpose(tp[:, i * P:(i + 1) * P], span(p, u, (j0 + i) * P, (j0 + i + 1) * P), ident[:])
                last.then_inc(sem("transposed"), 1)
                if k >= 1:
                    pe_values(pe, m, p, k - 1, turn)

        def pe_out(pe, m, q):
            k = [i for i, (u, _, _) in enumerate(GROUPS) if u // 4 == q][-1]
            pe.wait_ge(sem("ot"), NQ * m + q + 1 + 1)
            done = [i for i, (u, _, _) in enumerate(GROUPS) if u <= min(4 * q + 5, NU - 1)][-1]
            pe.wait_ge(sem("exp2"), NG * m + done + 1)
            for i in range(4):
                last = pe.transpose(tp[:, i * P:(i + 1) * P], ot[q % 2][:, i * P:(i + 1) * P], ident[:])
            last.then_inc(sem("rows"), 1)

        def pe_step(pe, front, back, p, turn, bturn):
            for s in range(NU + LAG + 1):
                if back is not None and s - LAG >= 0 and s - LAG < NU:
                    u = s - LAG
                    pe_back_scores(pe, back, 1 - p, u)
                if front is not None and s < NU:
                    pe_front(pe, front, p, s, turn)
                u = s - LAG - 1
                if back is not None and 0 <= u < NU:
                    pe_back_products(pe, back, 1 - p, u, bturn)
                    if u % 4 == 1 and u > 4:
                        pe_out(pe, back, u // 4 - 1)
            if back is not None:
                pe_values(pe, back, 1 - p, NG - 1, bturn)
                pe_out(pe, back, NQ - 1)

        def act_step(act, front, back, p, turn, bturn):
            bp = 1 - p
            if back is not None:
                for g in range(G):
                    act.wait_ge(sem("clipped"), NU * back + NB * (g + 1))
                    act.activation(xe[bp][:, g, :], xe[bp][:, g, :], ACT.Sqrt).then_inc(sem("dist"), 1)
                for g in range(G):
                    act.wait_ge(sem("dist"), G * back + g + 1)
                    if g == 0:
                        act.wait_ge(sem(f"v_loaded{bp}"), 32 * bturn + 32)
                    act.activation(xe[bp][:, g, :], xe[bp][:, g, :], ACT.Exp, scale=par[bp][:, g, 0:1]).then_inc(sem("effect"), 1)
            for s in range(NU + LAG + 1):
                if front is not None and s < NU:
                    act.wait_ge(sem("negmax"), NU * front + s + 1)
                    act.activation(span(p, s), s1[s % 2][:, 0:width(s)], ACT.Exp, bias=negmax[:, p, s:s + 1]).then_inc(sem("exp1"), 1)
                u = s - LAG - 1
                if back is not None and 0 <= u < NU:
                    for k, (gu, j0, n) in enumerate(GROUPS):
                        if gu != u:
                            continue
                        act.wait_ge(sem("transposed"), NG * back + k + 1)
                        if k >= 2:
                            act.wait_ge(sem("products"), NG * back + k - 1)
                        act.activation(pt[k % 2][:, 0:n * P], tp[:, 0:n * P], ACT.Exp, scale=-1.0).then_inc(sem("exp2"), 1)

        def dve_out(dve, m, q):
            dve.wait_ge(sem("rows"), NQ * m + q + 1)
            if q == 0:
                dve.wait_ge(sem("o_stored"), 16 * m + 1)
            for i in range(4):
                g, qb = UNITS[4 * q + i]
                dve.tensor_reduce(o[:, g, qb, :], tp[:, i * P:(i + 1) * P].rearrange("p (j d) -> p d j", d=32)[:, 0:VW, 0:min(4, qb + 1)],
                                  AX.X, ALU.add).then_inc(sem("o"), 1)

        def dve_ot(dve, m, q):
            k = [i for i, (u, _, _) in enumerate(GROUPS) if u // 4 == q][-1]
            dve.wait_ge(sem("products"), NG * m + k + 1)
            dve.tensor_copy(ot[q % 2][:], op[:]).then_inc(sem("ot"), 1)

        def dve_step(dve, front, back, p, turn, bturn):
            bp = 1 - p
            for s in range(NU + LAG + 3):
                if front is not None and s < NU:
                    dve.wait_ge(sem("scores1"), NU * front + s + 1)
                    dve.tensor_reduce(negmax[:, p, s:s + 1], s1[s % 2][:, 0:width(s)], AX.X, ALU.max, negate=True).then_inc(sem("negmax"), 1)
                u = s - LAG
                if back is not None and 0 <= u < NU:
                    dve.wait_ge(sem("scores2"), NU * back + u + 1)
                    if u % NB == 0:
                        dve.wait_ge(sem("effect"), G * back + UNITS[u][0] + 1)
                    alone(dve, sem)
                    dve.tensor_tensor_reduce(out=span(bp, u), in0=span(bp, u), in1=s2[:, 0:width(u)], scale=1.0, scalar=-3.4e38,
                                             op0=ALU.mult, op1=ALU.max, accum_out=max2[:, bp, u:u + 1]).then_inc(sem("weighted"), 1)
                u = s - 1
                if front is not None and 0 <= u < NU:
                    w = width(u)
                    g, qb = UNITS[u]
                    dve.wait_ge(sem("exp1"), NU * front + u + 1)
                    x = xe[p][:, g, :]
                    hi = OFF[qb] + w - 1
                    lo = OFF[qb] - 1
                    odd = x[:, hi:lo if lo >= 0 else None:-2]
                    even = x[:, hi - 1:lo if lo >= 0 else None:-2]
                    t = tail(u, 0)[:, ::-1]
                    dve.tensor_tensor_scan(t, odd, even, 0.0, ALU.add, ALU.add).then_inc(sem("scan"), 1)
                    dve.wait_ge(sem("scan"), NU * front + u + 1)
                    dve.reciprocal(rtot[:, p, u:u + 1], tail(u, 0)[:, 0:1]).then_inc(sem("rtot"), 1)
                u = s - 2
                if front is not None and 0 <= u < NU:
                    w = width(u)
                    if not POOL_ODD(u):
                        dve.wait_ge(sem("added"), NU * front + u + 1)
                        dve.tensor_tensor(plane(p, u, 1), tail(u, 1), pos[:, T - w + 1:T:2], ALU.mult).then_inc(sem("far_odd"), 1)
                    if u == 0:
                        dve.wait_ge(sem(f"v_loaded{p}"), 32 * turn + 32)
                    dve.wait_ge(sem("rtot"), NU * front + u + 1)
                    if not POOL_ODD(u):
                        dve.wait_ge(sem("far_odd"), NODD * front + sum(not POOL_ODD(v) for v in range(u + 1)))
                    dve.wait_ge(sem("far"), NU * front + u + 1)
                    dve.tensor_scalar(span(p, u), span(p, u), rtot[:, p, u:u + 1], par[p][:, UNITS[u][0], 1:2],
                                      ALU.mult, ALU.min).then_inc(sem("clipped"), 1)
                u = s - LAG - 1
                if back is not None and 0 <= u < NU:
                    if u % 4 == 0 and u > 0:
                        dve_ot(dve, back, u // 4 - 1)
                    if u % 4 == 1 and u > 4:
                        dve_out(dve, back, u // 4 - 1)
            if back is not None:
                dve_ot(dve, back, NQ - 1)
                dve_out(dve, back, NQ - 1)

        def pool_step(pool, front, back, p, turn, bturn):
            bp = 1 - p
            for s in range(NU + LAG + 3):
                u = s - 1
                if front is not None and 0 <= u < NU:
                    pool.wait_ge(sem("scan"), NU * front + u + 1)
                    pool.tensor_tensor(plane(p, u, 0), tail(u, 1), plane(p, u, 1), ALU.add).then_inc(sem("added"), 1)
                    w = width(u)
                    pool.wait_ge(sem("added"), NU * front + u + 1)
                    if POOL_ODD(u):
                        pool.tensor_tensor(plane(p, u, 1), tail(u, 1), pos[:, T - w + 1:T:2], ALU.mult)
                    pool.tensor_tensor(plane(p, u, 0), plane(p, u, 0), pos[:, T - w:T:2], ALU.mult).then_inc(sem("far"), 1)
                u = s - LAG
                if back is not None and 0 <= u < NU:
                    pool.wait_ge(sem("weighted"), NU * back + u + 1 + 1)
                    alone(pool, sem)
                    pool.tensor_scalar(span(bp, u), span(bp, u), -1.0, max2[:, bp, u:u + 1], ALU.mult, ALU.add).then_inc(sem("shifted"), 1)

        def loads(sp, m, p, first=False):
            for g in range(G):
                if not first:
                    sp.wait_ge(sem("scores2"), m * NU - 2 * NU + NB * (g + 1))
                head = st["qk"][DS((m * G + g) * DK, DK)].rearrange("d w r t -> w r d t")
                for r in range(NPART):
                    to = slice(r * NPART * DK, (r + 1) * NPART * DK)
                    sp.dma_start(qs[p][g][to, :], head[0, r].unsqueeze(0).to_broadcast([NPART, DK, T])).then_inc(sem(f"qk_loaded{g}{p}"), 16)
                    sp.dma_start(ks[p][g][to, :], head[1]).then_inc(sem(f"qk_loaded{g}{p}"), 16)
            if not first:
                sp.wait_ge(sem("products"), m * NG - NG)
            sp.dma_start(vals[p][:], st["v"][DS(m, 1)].rearrange("a p n w -> (a p) n w")).then_inc(sem(f"v_loaded{p}"), 16)
            sp.dma_start(par[p][:], st["par"][DS(m, 1)].rearrange("a p g k -> (a p) g k")).then_inc(sem(f"v_loaded{p}"), 16)

        def store(sp, m):
            sp.wait_ge(sem("o"), NU * m + NU + 1)
            sp.dma_start(st["o"][DS(m, 1)].rearrange("a p w -> (a p) w"), o[:].rearrange("p g n d -> p (g n d)")).then_inc(sem("o_stored"), 16)

        def steps(eng, step):
            step(eng, 0, None, 0, 0, None)
            with eng.Fori(0, (NSTEP - 2) // 2) as i:
                step(eng, i * 2 + 1, i * 2, 1, i, i)
                step(eng, i * 2 + 2, i * 2 + 1, 0, i + 1, i)
            step(eng, NSTEP - 1, NSTEP - 2, 1, NSTEP // 2 - 1, NSTEP // 2 - 1)
            step(eng, None, NSTEP - 1, 0, None, NSTEP // 2 - 1)

        with nc.Block() as block:
            @block.sync
            def _(sp):
                sp.sem_inc(sem("o_stored"), 1)
                sp.wait_ge(sem("pads"), 4 * G)
                loads(sp, 0, 0, first=True)
                loads(sp, 1, 1, first=True)
                with sp.Fori(0, (NSTEP - 2) // 2) as i:
                    loads(sp, i * 2 + 2, 0)
                    store(sp, i * 2)
                    loads(sp, i * 2 + 3, 1)
                    store(sp, i * 2 + 1)
                store(sp, NSTEP - 2)
                store(sp, NSTEP - 1)
                sp.wait_ge(sem("o_stored"), 16 * NSTEP + 1)

            @block.gpsimd
            def _(pool):
                steps(pool, pool_step)

            @block.vector
            def _(dve):
                for p in range(2):
                    for g in range(G):
                        dve.memset(qs[p][g][D:KP, :], 0.0).then_inc(sem("pads"), 1)
                        dve.memset(ks[p][g][D:KP, :], 0.0).then_inc(sem("pads"), 1)
                dve.memset(op[:], 0.0).then_inc(sem("cleared"), 1)
                dve.memset(behind[:, :, T // 2:T // 2 + 1], 0.0).then_inc(sem("cleared"), 1)
                dve.sem_inc(sem("weighted"), 1)
                dve.sem_inc(sem("ot"), 1)
                dve.sem_inc(sem("o"), 1)
                steps(dve, dve_step)

            @block.scalar
            def _(act):
                steps(act, act_step)

            @block.tensor
            def _(pe):
                pe.wait_ge(sem("cleared"), 2)
                steps(pe, pe_step)


def channel_phase(nc, a, st, hold, out):
    ident = hold["ident"]
    with ExitStack() as c:
        sb = lambda n, s, d=F32: c.enter_context(nc.sbuf_tensor(n, s, d))
        names = {}

        def sem(n):
            if n not in names:
                names[n] = c.enter_context(nc.semaphore("c_" + n))
            return names[n]

        NC = E * HID // P
        ow, rw = sb("ow", [KP, D]), sb("rw", [KP, E])
        w1 = sb("w1", [KP, E * HID])
        w2 = sb("w2", [P, NC, D])
        b2 = sb("b2", [KP, D])
        expandf = sb("expandf", [KP, E * HID])
        expand = sb("expand", [KP, E * HID], BF16)
        prio = sb("prio", [P, E])
        rowmask = sb("rowmask", [P, 1])
        eps = sb("eps5", [P, 1])
        os_ = sb("os", [P, H, NB, VW])
        rden = sb("rden", [P, H, NB])
        att = sb("att", [P, NB, H, DK])
        aT = sb("aT", [KP, T])
        h1 = sb("h1c", [P, NB, D])
        res = sb("res", [P, NB, D])
        xc, sq = sb("xc2", [P, NB, D]), sb("sq2", [P, NB, D])
        stat = sb("stat2", [P, 4, NB])
        h2 = sb("h2", [P, NB, D])
        h2T = sb("h2T", [KP, T])
        best = sb("best", [P, 2, NB])
        hot = sb("hot", [P, NB, E])
        rank = sb("rank", [P, NB, E])
        hotT = sb("hotT", [KP, T])
        coldT = sb("coldT", [KP, T], BF16)
        hid = sb("hid", [P, 2, T])
        fT = sb("fT", [D, T])
        y = sb("y", [P, NB, D])
        q0, q1, q2, q3 = (c.enter_context(nc.psum_tensor(f"pc{i}", [P, T], F32)) for i in range(4))
        half = lambda t, i: t[:, i * 512:(i + 1) * 512]
        blk = lambda t, i, w=P: t[:, i * w:(i + 1) * w]
        rows = lambda t: t.rearrange("p (n d) -> p n d", d=D)

        def norm_first(dve, x, n):
            dve.tensor_reduce(stat[:, 0, :], x, AX.X, ALU.add).then_inc(sem("ln"), 1)
            dve.wait_ge(sem("ln"), n + 1)
            dve.tensor_scalar(stat[:, 1, :], stat[:, 0, :], -1.0 / D, None, ALU.mult).then_inc(sem("ln"), 1)
            dve.wait_ge(sem("ln"), n + 2)
            dve.tensor_tensor(xc[:], x, stat[:, 1, :].unsqueeze(2).to_broadcast([P, NB, D]), ALU.add).then_inc(sem("ln"), 1)
            dve.wait_ge(sem("ln"), n + 3)
            dve.tensor_tensor(sq[:], xc[:], xc[:], ALU.mult).then_inc(sem("ln"), 1)
            dve.wait_ge(sem("ln"), n + 4)
            dve.tensor_reduce(stat[:, 2, :], sq[:], AX.X, ALU.add).then_inc(sem("var"), 1)

        def norm_second(dve, to, n, nstd, done):
            dve.wait_ge(sem("std"), nstd)
            dve.reciprocal(stat[:, 1, :], stat[:, 3, :]).then_inc(sem("ln"), 1)
            dve.wait_ge(sem("ln"), n + 5)
            dve.tensor_tensor(to, xc[:], stat[:, 1, :].unsqueeze(2).to_broadcast([P, NB, D]), ALU.mult).then_inc(done, 1)

        with nc.Block() as block:
            @block.sync
            def _(sp):
                for t, n in ((ow, "ow"), (rw, "rw"), (w1, "w1"), (w2, "w2"), (b2, "b2"), (expandf, "c_expand"),
                             (prio, "c_prio"), (rowmask, "c_rowmask"), (eps, "c_eps5")):
                    sp.dma_start(t[:], a[n]).then_inc(sem("weights"), 16)
                sp.sem_inc(sem("stored"), 1)
                with sp.Fori(0, B) as b:
                    sp.wait_ge(sem("att"), b + 1)
                    sp.dma_start(os_[:].rearrange("p (s g) n d -> p s (g n d)", g=G),
                                 st["o"][DS(b * HP, HP)].rearrange("s p w -> p s w")).then_inc(sem("o_loaded"), 16)
                    sp.wait_ge(sem("res"), b + 1)
                    sp.dma_start(h1[:], st["h1"][DS(b, 1)].rearrange("a p n d -> (a p) n d")).then_inc(sem("h1_loaded"), 16)
                    sp.wait_ge(sem("y"), b + 1)
                    sp.dma_start(out[DS(b, 1)].rearrange("a (n p) d -> (a p) n d", p=P), y[:]).then_inc(sem("stored"), 16)
                sp.wait_ge(sem("stored"), 16 * B + 1)

            @block.vector
            def _(dve):
                for t in (aT, h2T):
                    dve.memset(t[D:KP, :], 0.0).then_inc(sem("pads"), 1)
                dve.memset(hotT[:], 0.0).then_inc(sem("pads"), 1)
                dve.memset(coldT[:], 0.0).then_inc(sem("pads"), 1)
                dve.wait_ge(sem("pads"), 4)
                dve.memset(aT[D:D + 1, :], 1.0).then_inc(sem("pads"), 1)
                dve.memset(h2T[D:D + 1, :], 1.0).then_inc(sem("pads"), 1)
                dve.wait_ge(sem("weights"), 16 * 9)
                dve.tensor_copy(expand[:], expandf[:]).then_inc(sem("expand"), 1)
                dve.sem_inc(sem("att"), 1)
                dve.sem_inc(sem("res"), 1)
                dve.sem_inc(sem("res2"), 1)
                dve.wait_ge(sem("pads"), 6)
                with dve.Fori(0, B) as b:
                    dve.wait_ge(sem("o_loaded"), 16 * b + 16)
                    dve.reciprocal(rden[:], os_[:, :, :, DK]).then_inc(sem("rden"), 1)
                    dve.wait_ge(sem("rden"), 2 * b + 1)
                    dve.tensor_scalar(rden[:, :, 0], rden[:, :, 0], rowmask[:, 0:1], None, ALU.mult).then_inc(sem("rden"), 1)
                    dve.wait_ge(sem("rden"), 2 * b + 2)
                    dve.tensor_tensor(att[:].rearrange("p n h d -> p h n d"), os_[:, :, :, 0:DK],
                                      rden[:].unsqueeze(3).to_broadcast([P, H, NB, DK]), ALU.mult).then_inc(sem("att"), 1)
                    dve.wait_ge(sem("attended"), b + 1)
                    dve.wait_ge(sem("h1_loaded"), 16 * b + 16)
                    dve.tensor_tensor(res[:], rows(q1[:, 0:512]), h1[:], ALU.add).then_inc(sem("res"), 1)
                    dve.wait_ge(sem("res"), b + 1 + 1)
                    norm_first(dve, res[:], 10 * b)
                    norm_second(dve, h2[:], 10 * b, 2 * b + 1, sem("h2"))
                    dve.wait_ge(sem("logits"), b + 1)
                    logits = q1[:, 512:512 + NB * E].rearrange("p (n e) -> p n e", e=E)
                    dve.tensor_reduce(best[:, 0, :], logits, AX.X, ALU.max).then_inc(sem("hot"), 1)
                    dve.wait_ge(sem("hot"), 5 * b + 1)
                    dve.tensor_tensor(rank[:], logits, best[:, 0, :].unsqueeze(2).to_broadcast([P, NB, E]), ALU.is_ge).then_inc(sem("hot"), 1)
                    dve.wait_ge(sem("hot"), 5 * b + 2)
                    dve.tensor_tensor(rank[:], rank[:], prio[:].unsqueeze(1).to_broadcast([P, NB, E]), ALU.mult).then_inc(sem("hot"), 1)
                    dve.wait_ge(sem("hot"), 5 * b + 3)
                    dve.tensor_reduce(best[:, 1, :], rank[:], AX.X, ALU.max).then_inc(sem("hot"), 1)
                    dve.wait_ge(sem("hot"), 5 * b + 4)
                    dve.tensor_tensor(hot[:], rank[:], best[:, 1, :].unsqueeze(2).to_broadcast([P, NB, E]), ALU.is_equal).then_inc(sem("hot"), 1)
                    dve.wait_ge(sem("hotT_ps"), b + 1)
                    dve.tensor_copy(hotT[0:E, :], q2[0:E, :]).then_inc(sem("hotT"), 1)
                    dve.wait_ge(sem("hotT"), b + 1)
                    dve.tensor_scalar(coldT[0:E, :], hotT[0:E, :], -1.0, None, ALU.add).then_inc(sem("coldT"), 1)
                    dve.wait_ge(sem("experts"), b + 1)
                    dve.tensor_tensor(res[:], rows(q1[:, 0:512]), h2[:], ALU.add).then_inc(sem("res2"), 1)
                    dve.wait_ge(sem("res2"), b + 1 + 1)
                    norm_first(dve, res[:], 10 * b + 5)
                    dve.wait_ge(sem("stored"), 16 * b + 1)
                    norm_second(dve, y[:], 10 * b + 5, 2 * b + 2, sem("y"))

            @block.scalar
            def _(act):
                act.wait_ge(sem("weights"), 16 * 9)
                act.wait_ge(sem("pads"), 6)
                with act.Fori(0, B) as b:
                    act.wait_ge(sem("aT_ps"), b + 1)
                    act.copy(aT[0:D, :], q0[0:D, :]).then_inc(sem("aT"), 1)
                    act.wait_ge(sem("var"), 2 * b + 1)
                    act.activation(stat[:, 3, :], stat[:, 2, :], ACT.Sqrt, scale=1.0 / D, bias=eps[:, 0:1]).then_inc(sem("std"), 1)
                    act.wait_ge(sem("h2T_ps"), b + 1)
                    act.copy(h2T[0:D, :], q0[0:D, :]).then_inc(sem("h2T"), 1)
                    for i in range(NC):
                        act.wait_ge(sem("hidden"), NC * b + i + 1)
                        if i >= 2:
                            act.wait_ge(sem("mixed"), NC * b + i - 1)
                        act.activation(hid[:, i % 2, :], (q3, q0)[i % 2][:], ACT.Relu).then_inc(sem("relu"), 1)
                    act.wait_ge(sem("mixed"), NC * b + NC)
                    act.activation(fT[:], q2[0:D, :], ACT.Relu).then_inc(sem("fT"), 1)
                    act.wait_ge(sem("var"), 2 * b + 2)
                    act.activation(stat[:, 3, :], stat[:, 2, :], ACT.Sqrt, scale=1.0 / D, bias=eps[:, 0:1]).then_inc(sem("std"), 1)

            @block.tensor
            def _(pe):
                mm = pe.matmul
                pe.wait_ge(sem("weights"), 16 * 9)
                pe.wait_ge(sem("pads"), 6)
                pe.wait_ge(sem("expand"), 1)
                with pe.Fori(0, B) as b:
                    pe.wait_ge(sem("att"), b + 1 + 1)
                    alone(pe, sem)
                    for n in range(NB):
                        last = pe.transpose(blk(q0, n)[0:D, :], att[:, n].rearrange("p h d -> p (h d)"), ident[:])
                    last.then_inc(sem("aT_ps"), 1)
                    pe.wait_ge(sem("aT"), b + 1)
                    pe.wait_ge(sem("res2"), b + 1)
                    for n in range(NB):
                        last = mm(blk(q1, n, D), blk(aT, n), ow[:], start=True, stop=True)
                    last.then_inc(sem("attended"), 1)
                    pe.wait_ge(sem("h2"), b + 1)
                    alone(pe, sem)
                    for n in range(NB):
                        last = pe.transpose(blk(q0, n)[0:D, :], h2[:, n, :], ident[:])
                    last.then_inc(sem("h2T_ps"), 1)
                    pe.wait_ge(sem("h2T"), b + 1)
                    for n in range(NB):
                        last = mm(q1[:, 512 + n * E:512 + (n + 1) * E], blk(h2T, n), rw[:], start=True, stop=True)
                    last.then_inc(sem("logits"), 1)
                    pe.wait_ge(sem("hot"), 5 * b + 5)
                    alone(pe, sem)
                    for n in range(NB):
                        last = pe.transpose(blk(q2, n)[0:E, :], hot[:, n, :], ident[:])
                    last.then_inc(sem("hotT_ps"), 1)
                    pe.wait_ge(sem("coldT"), b + 1)
                    for i in range(NC + 1):
                        if i < NC:
                            if i >= 2:
                                pe.wait_ge(sem("relu"), NC * b + i - 1)
                            for n in range(2):
                                dst = half((q3, q0)[i % 2], n)
                                mm(dst, blk(w1, i), half(h2T, n), start=True, stop=False)
                                last = mm(dst, blk(expand, i), half(coldT, n), start=False, stop=True)
                            last.then_inc(sem("hidden"), 1)
                        if i == 1:
                            pe.wait_ge(sem("hotT"), b + 1)
                            for n in range(2):
                                mm(half(q2, n)[0:D, :], b2[:], half(hotT, n), start=True, stop=False)
                        if i >= 1:
                            pe.wait_ge(sem("relu"), NC * b + i)
                            for n in range(2):
                                last = mm(half(q2, n)[0:D, :], w2[:, i - 1, :], hid[:, (i - 1) % 2, n * 512:(n + 1) * 512],
                                          start=False, stop=i == NC)
                            last.then_inc(sem("mixed"), 1)
                    pe.wait_ge(sem("fT"), b + 1)
                    alone(pe, sem)
                    for n in range(NB):
                        last = pe.transpose(blk(q1, n, D), fT[:, blk_of(n)], ident[0:D, 0:D])
                    last.then_inc(sem("experts"), 1)


def blk_of(n):
    return slice(n * P, (n + 1) * P)


def program(nc, a, out):
    st = {
        "par": nc.dram_tensor("step_par", [NSTEP, P, G, 2], F32).ap(),
        "h1": nc.dram_tensor("tok_rows", [B, P, NB, D], F32).ap(),
        "v": nc.dram_tensor("value_rows", [NSTEP, P, NB, G * VW], F32).ap(),
        "qk": nc.dram_tensor("qk_parts", [B * H * DK, 2, NPART, T], BF16).ap(),
        "o": nc.dram_tensor("attended_rows", [NSTEP, P, G * NB * VW], F32).ap(),
    }
    with ExitStack() as c:
        hold = {
            "ident": c.enter_context(nc.sbuf_tensor("ident", [P, P], F32)),
            "identb": c.enter_context(nc.sbuf_tensor("identb", [P, P], BF16)),
            "maskb": c.enter_context(nc.sbuf_tensor("maskb", [P, P], BF16)),
            "pos": c.enter_context(nc.sbuf_tensor("pos", [P, T], F32)),
            "gam": c.enter_context(nc.sbuf_tensor("gam", [P, H], F32)),
        }
        setup_phase(nc, a, st, hold)
        token_phase(nc, a, st, hold)
        attention_phase(nc, a, st, hold)
        channel_phase(nc, a, st, hold, out)


def kernel(**inputs):
    import numpy as np
    import concourse.bacc as bacc
    from concourse.bass_utils import run_bass_kernel_spmd

    f = np.float32
    i = {n: np.asarray(x) for n, x in inputs.items()}
    tok, att, ffn = ({n[len(k):]: x for n, x in i.items() if n.startswith(k)} for k in ("L0_tok_", "L0_attn_", "L0_ffn_"))

    def padded(rows, *parts):
        parts = [p.reshape(-1, p.shape[-1]) for p in parts]
        return np.concatenate(parts + [np.zeros((rows - sum(len(p) for p in parts), parts[0].shape[1]), f)], 0)

    wva = np.zeros((D + 1, H, VW), f)
    wva[:D, :, :DK] = att["v_w"].T.reshape(D, H, DK)
    wva[D, :, :DK] = att["v_b"].reshape(H, DK)
    wva[D, :, DK] = 1.0
    taps = att["conv_w"].transpose(2, 1, 0)
    cw = np.zeros((P, 3, D), f)
    for k in range(TAPS):
        cw[D * (k % 2):D * (k % 2) + D, k // 2] = taps[k]
    r, x = np.arange(P)[:, None], np.arange(T)[None, :]
    arrays = {
        "xT": i["x"].reshape(B, T, D).transpose(0, 2, 1),
        "gammaT": tok["d_gamma_batched"].T.reshape(NB, P, T).transpose(1, 0, 2),
        "wq": padded(KP, tok["Wq"], tok["bq"]), "wk": padded(KP, tok["Wk"], tok["bk"]), "wv": padded(KP, tok["Wv"], tok["bv"]),
        "wo2": np.concatenate([tok["Wo"], tok["Wo"]], 0),
        "bo_row": padded(KP, np.tile(tok["bo"], NB)),
        "cb_row": padded(KP, np.tile(att["conv_b"], NB)),
        "beta": np.repeat(att["sqrt_beta"].reshape(1, D), P, 0),
        "conv_w": cw,
        "prelu": np.repeat(tok["prelu_a"].reshape(1, 1), P, 0),
        "ln_wb": np.stack([att["ln_w"], att["ln_b"]], 1),
        "wqk": padded(KP, np.concatenate([att["q_w"].T, att["k_w"].T], 1), np.concatenate([att["q_b"], att["k_b"]])),
        "wva": padded(KP, wva.reshape(D + 1, H * VW)),
        "gammas": np.repeat(att["gammas"].reshape(1, H), P, 0),
        "ow": padded(KP, att["out_w"].T, att["out_b"]),
        "rw": padded(KP, ffn["router_w"].T, ffn["router_b"]),
        "w1": padded(KP, ffn["W1"].transpose(1, 0, 2).reshape(D, E * HID), ffn["b1"].reshape(1, E * HID)),
        "w2": ffn["W2"].reshape(E * HID // P, P, D).transpose(1, 0, 2),
        "b2": padded(KP, ffn["b2"]),
        "c_ident": np.eye(P, dtype=f),
        "c_mask": np.where(np.arange(P)[None, :] > r, f(MASKED), f(0)).astype(f),
        "c_pos": np.maximum(r + T - P - x, 0).astype(f),
        "c_ones_row": padded(KP, np.ones((1, P), f)),
        "c_eps12": np.full((P, 1), 1e-12, f), "c_eps5": np.full((P, 1), 1e-5, f),
        "c_qk_scale": np.concatenate([np.full((D, 1), DK ** -0.5, f), np.ones((D, 1), f)], 0),
        "c_expand": padded(KP, np.repeat(np.eye(E, dtype=f), HID, 1) * f(1e30)),
        "c_prio": np.repeat(np.arange(E, 0, -1, dtype=f)[None], P, 0),
        "c_rowmask": (r > 0).astype(f),
    }
    nc = bacc.Bacc("TRN2", target_bir_lowering=False, num_devices=1)
    arrays = {n: np.ascontiguousarray(x) for n, x in arrays.items()}
    a = {n: nc.dram_tensor("in_" + n, x.shape, mybir.dt.from_np(x.dtype), kind="ExternalInput").ap() for n, x in arrays.items()}
    out = nc.dram_tensor("out_rows", (B, T, D), F32, kind="ExternalOutput").ap()
    program(nc, a, out)
    got = run_bass_kernel_spmd(nc, [{"in_" + n: x for n, x in arrays.items()}], core_ids=[0])
    return got.results[0]["out_rows"]
```

```python
import math
from collections import namedtuple
from contextlib import ExitStack

import concourse.bass as bass
from concourse import mybir

ALU = mybir.AluOpType
ACT = mybir.ActivationFunctionType
AX = mybir.AxisListType
F32 = mybir.dt.float32
BF16 = mybir.dt.bfloat16
DS = bass.ds

P = 128
B, T, D = 16, 1024, 64
NB = T // P
H, DK = 8, 8
TAPS = 5
E, HID = 32, 16
KP = 96
NPART = 3
VW = DK + 1

G = 2
HP = H // G
NSTEP = B * HP
ORDER = (7, 0, 6, 1, 5, 2, 4, 3)
UNITS = [(g, qb) for g in range(G) for qb in ORDER]
NU = len(UNITS)
HEADW = sum(P * (qb + 1) for qb in range(NB))
WIDTH = [P * (qb + 1) for g, qb in UNITS]
START = [sum(WIDTH[:u]) for u in range(NU)]
TILES = [(u, j, min(4, qb + 1 - j)) for u, (g, qb) in enumerate(UNITS) for j in range(0, qb + 1, 4)]
NT = len(TILES)
NQ = NU // 4
MAX, EXP = 1, 2
SQRT_SLOT = 6
EFFECT = NU + SQRT_SLOT
SCORES2 = EFFECT + 1
WEIGH = SCORES2 + 1
SUM = WEIGH + 1
EXP2 = SUM + 1
NHELD = 5
BEHIND = 2
NPT = 3
NBEHIND = 8
HELD = range(SQRT_SLOT - 2 - NHELD + 1, SQRT_SLOT - 1)
SCAN = [SQRT_SLOT + 1 if u in HELD else u + 3 for u in range(NU)]
CLIP = [SQRT_SLOT + 1 + (u - HELD[0]) // 2 if u in HELD else u + 5 for u in range(NU)]
MASKED = -1e32
LN_FLOOR = math.log(1e-5)

Group = namedtuple("Group", "n p turn")


def POOL_ODD(u):
    return u % 2 == 0


NODD = sum(not POOL_ODD(u) for u in range(NU))


def ACT_SHIFT(u):
    return u % 4 == 0


def first(m):
    return isinstance(m.n, int) and m.n == 0


def last(m):
    return isinstance(m.n, int) and m.n == NSTEP - 1


def tiles_of(u):
    return [k for k, tile in enumerate(TILES) if tile[0] == u]


def rows_bank(q):
    return (tiles_of((4 * q + 5) % NU)[-1] + 1) % 2


def head(t, g):
    return t[:, g * HEADW:(g + 1) * HEADW]


def alone(eng, sem):
    eng.sem_inc(sem("passed"), 1)


def setup_phase(nc, a, st, hold):
    ident, identb, maskb, pos, gam = hold["ident"], hold["identb"], hold["maskb"], hold["pos"], hold["gam"]
    with ExitStack() as c:
        sb = lambda n, s, d=F32: c.enter_context(nc.sbuf_tensor(n, s, d))
        sem = lambda n: c.enter_context(nc.semaphore(n))
        maskf = sb("maskf", [P, P])
        e = sb("gam_exp", [P, 4, H])
        par = sb("par", [P, 2, H])
        loaded, ab, ex, ln, sp, stored, rc = (sem("set_" + n) for n in
                                              ("loaded", "abs", "exp", "ln", "sp", "stored", "rc"))
        conv = sem("set_conv")
        with nc.Block() as block:
            @block.sync
            def _(sp_):
                sp_.dma_start(ident[:], a["c_ident"]).then_inc(loaded, 16)
                sp_.dma_start(maskf[:], a["c_mask"]).then_inc(loaded, 16)
                sp_.dma_start(pos[:], a["c_pos"]).then_inc(loaded, 16)
                sp_.dma_start(gam[:], a["gammas"]).then_inc(loaded, 16)
                sp_.wait_ge(sp, 4)
                with sp_.Fori(0, B) as b:
                    for s in range(HP):
                        for k in range(2):
                            sp_.dma_start(st["par"][DS(b * HP + s, 1), k].rearrange("a p g -> (a p) g"),
                                          par[:, k, s * G:(s + 1) * G]).then_inc(stored, 16)
                sp_.wait_ge(stored, 16 * 2 * NSTEP)

            @block.vector
            def _(dve):
                dve.wait_ge(loaded, 64)
                dve.tensor_copy(identb[:], ident[:]).then_inc(conv, 1)
                dve.tensor_copy(maskb[:], maskf[:]).then_inc(conv, 1)
                dve.scalar_tensor_tensor(e[:, 0], gam[:], -1.0, gam[:], ALU.mult, ALU.max).then_inc(ab, 1)
                dve.wait_ge(ln, 1)
                dve.scalar_tensor_tensor(e[:, 3], gam[:], 0.0, e[:, 2], ALU.max, ALU.add).then_inc(sp, 1)
                dve.wait_ge(sp, 1)
                dve.tensor_scalar(par[:, 0], e[:, 3], -1.0, None, ALU.mult).then_inc(sp, 1)
                dve.reciprocal(e[:, 0], e[:, 3]).then_inc(sp, 1)
                dve.wait_ge(sp, 3)
                dve.scalar_tensor_tensor(par[:, 1], e[:, 0], LN_FLOOR ** 2, e[:, 0], ALU.mult, ALU.mult).then_inc(sp, 1)

            @block.scalar
            def _(act):
                act.wait_ge(ab, 1)
                act.activation(e[:, 1], e[:, 0], ACT.Exp, scale=-1.0).then_inc(ex, 1)
                act.wait_ge(ex, 1)
                act.activation(e[:, 2], e[:, 1], ACT.Ln, bias=1.0).then_inc(ln, 1)


def token_phase(nc, a, st, hold):
    ident = hold["ident"]
    with ExitStack() as c:
        sb = lambda n, s, d=F32: c.enter_context(nc.sbuf_tensor(n, s, d))
        names = {}

        def sem(n):
            if n not in names:
                names[n] = c.enter_context(nc.semaphore("a_" + n))
            return names[n]

        gammaT = sb("gammaT", [P, NB, T])
        xT = sb("xT", [KP, T])
        wq, wk, wv = sb("wq", [KP, D]), sb("wk", [KP, D]), sb("wv", [KP, D])
        wo2 = sb("wo2", [P, D])
        bo_row, cb_row, ones_row = sb("bo_row", [KP, NB * D]), sb("cb_row", [KP, NB * D]), sb("ones_row", [KP, P])
        beta = sb("beta", [P, D])
        beta2 = sb("beta2", [P, 2, D])
        cw = sb("cw", [P, 3, D])
        prelu = sb("prelu", [P, 1])
        eps = sb("eps", [P, 1])
        ln_wb = sb("ln_wb", [D, 2])
        wqk = sb("wqk", [KP, 2 * D])
        wva = sb("wva", [KP, H * VW])
        qk_scale = sb("qk_scale", [P, 1])
        qT, kT = sb("qT", [KP, T]), sb("kT", [KP, T])
        v = sb("v", [P, NB, D])
        gm = sb("gm", [P, 2, T])
        retT = sb("retT", [P, T])
        neg = sb("neg", [P, NB, D])
        h1 = sb("h1", [P, NB, 2, D])
        hT = sb("hT", [P, T + 4])
        stat = sb("stat", [P, 4, NB])
        xc, sq = sb("xc", [P, NB, D]), sb("sq", [P, NB, D])
        nT = sb("nT", [KP, T])
        qk = sb("qk", [P, T])
        rest = sb("rest", [P, T])
        part = sb("part", [P, NPART, T], BF16)
        va = sb("va", [P, NB, H * VW])
        p0, p1, p2, p3 = (c.enter_context(nc.psum_tensor(f"pa{i}", [P, T], F32)) for i in range(4))
        half = lambda t, i: t[:, i * 512:(i + 1) * 512]
        blk = lambda t, i, w=P: t[:, i * w:(i + 1) * w]

        with nc.Block() as block:
            @block.sync
            def _(sp):
                for t, n in ((gammaT, "gammaT"), (wq, "wq"), (wk, "wk"), (wv, "wv"), (wo2, "wo2"), (bo_row, "bo_row"),
                             (cb_row, "cb_row"), (ones_row, "c_ones_row"), (beta, "beta"), (cw, "conv_w"),
                             (prelu, "prelu"), (eps, "c_eps12"), (ln_wb, "ln_wb"), (wqk, "wqk"), (wva, "wva"),
                             (qk_scale, "c_qk_scale")):
                    sp.dma_start(t[:], a[n]).then_inc(sem("weights"), 16)
                sp.sem_inc(sem("h1_stored"), 1)
                sp.sem_inc(sem("qk_stored"), 1)
                sp.sem_inc(sem("v_stored"), 1)
                with sp.Fori(0, B) as b:
                    sp.wait_ge(sem("v_proj"), b + 1)
                    sp.dma_start(xT[0:D, :], a["xT"][DS(b, 1)].rearrange("a d t -> (a d) t")).then_inc(sem("x_loaded"), 16)
                    sp.wait_ge(sem("h1"), b + 1)
                    sp.dma_start(st["h1"][DS(b, 1)].rearrange("a p n d -> (a p) n d"), h1[:, :, 0, :]).then_inc(sem("h1_stored"), 16)
                    sp.wait_ge(sem("va"), b + 1 + 1)
                    for s in range(HP):
                        sp.dma_start(st["v"][DS(b * HP + s, 1)].rearrange("a p n w -> (a p) n w"),
                                     va[:, :, s * G * VW:(s + 1) * G * VW]).then_inc(sem("v_stored"), 16)
                    sp.wait_ge(sem("part2"), b + 1)
                    for r in range(NPART):
                        for w in range(2):
                            sp.dma_start(st["qk"][DS(b * D, D), w, r], part[w * D:(w + 1) * D, r, :]).then_inc(sem("qk_stored"), 16)
                sp.wait_ge(sem("h1_stored"), 16 * B + 1)
                sp.wait_ge(sem("v_stored"), 16 * HP * B + 1)
                sp.wait_ge(sem("qk_stored"), 16 * 2 * NPART * B + 1)

            @block.gpsimd
            def _(pool):
                with pool.Fori(0, B) as b:
                    pool.wait_ge(sem("h1"), b + 1)
                    alone(pool, sem)
                    pool.tensor_copy(h1[:, :, 1, :], h1[:, :, 0, :]).then_inc(sem("h1_twice"), 1)
                    pool.wait_ge(sem("part0"), b + 1 + 1)
                    pool.tensor_tensor(rest[:], qk[:], part[:, 0, :], ALU.subtract).then_inc(sem("rest"), 1)

            @block.vector
            def _(dve):
                for t in (xT, nT, qT, kT):
                    dve.memset(t[D:KP, :], 0.0).then_inc(sem("pads"), 1)
                dve.memset(hT[:], 0.0).then_inc(sem("pads"), 1)
                dve.wait_ge(sem("pads"), 5)
                dve.memset(xT[D:D + 1, :], 1.0).then_inc(sem("pads"), 1)
                dve.memset(nT[D:D + 1, :], 1.0).then_inc(sem("pads"), 1)
                dve.wait_ge(sem("weights"), 16 * 16)
                dve.tensor_tensor(beta2[:, 0, :], beta[:], beta[:], ALU.mult).then_inc(sem("cw"), 1)
                dve.wait_ge(sem("cw"), 1)
                dve.tensor_scalar(beta2[:, 1, :], beta2[:, 0, :], 1.0, None, ALU.add).then_inc(sem("cw"), 1)
                dve.wait_ge(sem("cw"), 2)
                dve.tensor_scalar(beta2[:, 0, :], beta2[:, 0, :], -1.0, 1.0, ALU.mult, ALU.add).then_inc(sem("cw"), 1)
                dve.wait_ge(sem("cw"), 3)
                dve.tensor_tensor(cw[:], cw[:], beta2[:, 0:1, :].to_broadcast([P, 3, D]), ALU.mult).then_inc(sem("cw"), 1)
                dve.tensor_tensor(beta[0:D, :], ident[0:D, 0:D], beta2[0:D, 1, :], ALU.mult).then_inc(sem("cw"), 1)
                dve.wait_ge(sem("cw"), 5)
                dve.tensor_tensor(cw[0:D, 2, :], cw[0:D, 2, :], beta[0:D, :], ALU.add).then_inc(sem("cw"), 1)
                dve.tensor_tensor(cb_row[:].rearrange("p (n d) -> p n d", d=D), cb_row[:].rearrange("p (n d) -> p n d", d=D),
                                  beta2[0:KP, 0:1, :].to_broadcast([KP, NB, D]), ALU.mult).then_inc(sem("cw"), 1)
                dve.wait_ge(sem("pads"), 7)
                with dve.Fori(0, B) as b:
                    dve.wait_ge(sem("qk_proj"), 2 * b + 2)
                    dve.tensor_copy(kT[0:D, :], p1[0:D, :]).then_inc(sem("kT"), 1)
                    for s in range(NB):
                        dve.wait_ge(sem("scores"), NB * b + s + 1)
                        if s >= 2:
                            dve.wait_ge(sem("ret"), NB * b + s - 1)
                        dve.tensor_tensor(gm[:, s % 2, :], (p0, p1)[s % 2][:], gammaT[:, s, :], ALU.mult).then_inc(sem("gated"), 1)
                    dve.wait_ge(sem("y"), b + 1)
                    y = p2[:, 512:1024].rearrange("p (n d) -> p n d", d=D)
                    dve.tensor_scalar(neg[:], y, 0.0, prelu[:, 0:1], ALU.min, ALU.mult).then_inc(sem("neg"), 1)
                    dve.wait_ge(sem("neg"), b + 1)
                    dve.wait_ge(sem("h1_stored"), 16 * b + 1)
                    dve.scalar_tensor_tensor(h1[:, :, 0, :], y, 0.0, neg[:], ALU.max, ALU.add).then_inc(sem("h1"), 1)
                    dve.wait_ge(sem("h1T"), b + 1)
                    dve.tensor_copy(hT[D:P, 3:3 + T], p0[D:P, :]).then_inc(sem("hT_high"), 1)
                    dve.wait_ge(sem("z"), b + 1)
                    z = p1[:, 0:512].rearrange("p (n d) -> p n d", d=D)
                    dve.tensor_reduce(stat[:, 0, :], z, AX.X, ALU.add).then_inc(sem("ln"), 1)
                    dve.wait_ge(sem("ln"), 6 * b + 1)
                    dve.tensor_scalar(stat[:, 1, :], stat[:, 0, :], -1.0 / D, None, ALU.mult).then_inc(sem("ln"), 1)
                    dve.wait_ge(sem("ln"), 6 * b + 2)
                    dve.tensor_tensor(xc[:], z, stat[:, 1, :].unsqueeze(2).to_broadcast([P, NB, D]), ALU.add).then_inc(sem("ln"), 1)
                    dve.wait_ge(sem("ln"), 6 * b + 3)
                    dve.tensor_tensor(sq[:], xc[:], xc[:], ALU.mult).then_inc(sem("ln"), 1)
                    dve.wait_ge(sem("ln"), 6 * b + 4)
                    dve.tensor_reduce(stat[:, 2, :], sq[:], AX.X, ALU.add).then_inc(sem("var"), 1)
                    dve.wait_ge(sem("std"), b + 1)
                    dve.reciprocal(stat[:, 1, :], stat[:, 3, :]).then_inc(sem("ln"), 1)
                    dve.wait_ge(sem("ln"), 6 * b + 5)
                    dve.tensor_tensor(xc[:], xc[:], stat[:, 1, :].unsqueeze(2).to_broadcast([P, NB, D]), ALU.mult).then_inc(sem("ln"), 1)
                    dve.wait_ge(sem("rest"), b + 1)
                    dve.tensor_copy(part[:, 1, :], rest[:]).then_inc(sem("part1"), 1)
                    dve.wait_ge(sem("part1"), b + 1)
                    dve.tensor_tensor(part[:, 2, :], rest[:], part[:, 1, :], ALU.subtract).then_inc(sem("part2"), 1)

            @block.scalar
            def _(act):
                act.sem_inc(sem("part0"), 1)
                act.sem_inc(sem("va"), 1)
                act.wait_ge(sem("weights"), 16 * 16)
                act.wait_ge(sem("pads"), 7)
                with act.Fori(0, B) as b:
                    act.wait_ge(sem("qk_proj"), 2 * b + 1)
                    act.copy(qT[0:D, :], p0[0:D, :]).then_inc(sem("qT"), 1)
                    act.wait_ge(sem("v_proj"), b + 1 + 1)
                    act.copy(v[:].rearrange("p n d -> p (n d)"), p2[:, 0:512]).then_inc(sem("v"), 1)
                    act.wait_ge(sem("ret"), NB * b + NB)
                    act.copy(retT[:], p3[:]).then_inc(sem("retT"), 1)
                    act.wait_ge(sem("h1T"), b + 1)
                    act.copy(hT[0:D, 4:4 + T], p0[0:D, :]).then_inc(sem("hT_low"), 1)
                    act.wait_ge(sem("var"), b + 1)
                    act.activation(stat[:, 3, :], stat[:, 2, :], ACT.Sqrt, scale=1.0 / D, bias=eps[:, 0:1]).then_inc(sem("std"), 1)
                    act.wait_ge(sem("nT_ps"), b + 1)
                    act.activation(nT[0:D, :], p2[0:D, :], ACT.Identity, scale=ln_wb[:, 0:1], bias=ln_wb[:, 1:2]).then_inc(sem("nT"), 1)
                    act.wait_ge(sem("qk2"), b + 1)
                    act.wait_ge(sem("qk_stored"), 16 * 2 * NPART * b + 1)
                    act.activation(part[:, 0, :], p0[:], ACT.Copy, scale=qk_scale[:, 0:1]).then_inc(sem("part0_"), 1)
                    act.activation(qk[:], p0[:], ACT.Copy, scale=qk_scale[:, 0:1]).then_inc(sem("part0"), 1)
                    act.wait_ge(sem("va_ps"), b + 1)
                    act.wait_ge(sem("v_stored"), 16 * HP * b + 1)
                    act.copy(va[:], p1[:].rearrange("p (n w) -> p n w", w=P)[:, :, 0:H * VW]).then_inc(sem("va"), 1)

            @block.tensor
            def _(pe):
                mm = pe.matmul
                pe.sem_inc(sem("v_proj"), 1)
                pe.wait_ge(sem("weights"), 16 * 16)
                pe.wait_ge(sem("pads"), 7)
                pe.wait_ge(sem("cw"), 7)
                with pe.Fori(0, B) as b:
                    pe.wait_ge(sem("x_loaded"), 16 * b + 16)
                    pe.wait_ge(sem("part0"), b + 1)
                    pe.wait_ge(sem("va"), b + 1)
                    for w, p in ((wq, p0), (wk, p1)):
                        for n in range(2):
                            last = mm(half(p, n)[0:D, :], w[:], half(xT, n), start=True, stop=True)
                        last.then_inc(sem("qk_proj"), 1)
                    for n in range(NB):
                        last = mm(blk(p2, n, D), blk(xT, n), wv[:], start=True, stop=True)
                    last.then_inc(sem("v_proj"), 1)
                    pe.wait_ge(sem("qT"), b + 1)
                    pe.wait_ge(sem("kT"), b + 1)
                    for s in range(NB + 1):
                        if s < NB:
                            if s >= 2:
                                pe.wait_ge(sem("gated"), NB * b + s - 1)
                            for n in range(2):
                                last = mm(half((p0, p1)[s % 2], n), blk(kT, s), half(qT, n), start=True, stop=True)
                            last.then_inc(sem("scores"), 1)
                        if s >= 1:
                            t = s - 1
                            if t == 0:
                                pe.wait_ge(sem("v"), b + 1)
                            pe.wait_ge(sem("gated"), NB * b + t + 1)
                            r = D * (t % 2)
                            for n in range(2):
                                last = mm(half(p3, n)[r:r + D, :], v[:, t, :], gm[:, t % 2, n * 512:(n + 1) * 512],
                                          start=t < 2, stop=t >= NB - 2)
                            last.then_inc(sem("ret"), 1)
                    pe.wait_ge(sem("retT"), b + 1)
                    mm(p2[:, 512:1024], ones_row[:], bo_row[:], start=True, stop=False)
                    for n in range(NB):
                        last = mm(p2[:, 512 + n * D:512 + (n + 1) * D], blk(retT, n), wo2[:], start=False, stop=n == NB - 1)
                    last.then_inc(sem("y"), 1)
                    pe.wait_ge(sem("h1_twice"), b + 1)
                    for n in range(NB):
                        last = pe.transpose(blk(p0, n), h1[:, n].rearrange("p a d -> p (a d)"), ident[:])
                    last.then_inc(sem("h1T"), 1)
                    pe.wait_ge(sem("hT_low"), b + 1)
                    pe.wait_ge(sem("hT_high"), b + 1)
                    mm(p1[:, 0:512], ones_row[:], cb_row[:], start=True, stop=False)
                    for n in range(NB):
                        for k in range(3):
                            last = mm(p1[:, n * D:(n + 1) * D], hT[:, n * P + 2 * k:n * P + 2 * k + P], cw[:, k, :],
                                      start=False, stop=n == NB - 1 and k == 2)
                    last.then_inc(sem("z"), 1)
                    pe.wait_ge(sem("ln"), 6 * b + 6)
                    alone(pe, sem)
                    for n in range(NB):
                        last = pe.transpose(blk(p2, n)[0:D, :], xc[:, n, :], ident[:])
                    last.then_inc(sem("nT_ps"), 1)
                    pe.wait_ge(sem("nT"), b + 1)
                    for n in range(2):
                        last = mm(half(p0, n), wqk[:], half(nT, n), start=True, stop=True)
                    last.then_inc(sem("qk2"), 1)
                    for n in range(NB):
                        last = mm(p1[:, n * P:n * P + H * VW], blk(nT, n), wva[:], start=True, stop=True)
                    last.then_inc(sem("va_ps"), 1)


def attention_phase(nc, a, st, hold):
    ident, identb, maskb, pos = hold["ident"], hold["identb"], hold["maskb"], hold["pos"]
    with ExitStack() as c:
        sb = lambda n, s, d=F32: c.enter_context(nc.sbuf_tensor(n, s, d))
        names = {}

        def sem(n):
            if n not in names:
                names[n] = c.enter_context(nc.semaphore("b_" + n))
            return names[n]

        qs = [[sb(f"qs{p}{g}", [KP, T], BF16) for g in range(G)] for p in range(2)]
        ks = [[sb(f"ks{p}{g}", [KP, T], BF16) for g in range(G)] for p in range(2)]
        xe = [sb(f"xe{p}", [P, G * HEADW]) for p in range(2)]
        vals = [sb(f"vals{p}", [P, NB, G * VW]) for p in range(2)]
        limit = [sb(f"limit{p}", [P, G]) for p in range(2)]
        rate = [sb(f"rate{p}", [P, G]) for p in range(2)]
        negmax, rtot, max2 = sb("negmax", [P, 2, NU]), sb("rtot", [P, 2, NU]), sb("max2", [P, 2, NU])
        behind = sb("behind", [P, NBEHIND, T // 2 + 1])
        pt = [sb(f"pt{i}", [P, 512]) for i in range(NPT)]
        ot = [sb(f"ot{i}", [P, 512]) for i in range(2)]
        o = sb("o", [P, G, NB, VW])
        s1 = [c.enter_context(nc.psum_tensor(f"s1_{i}", [P, max(WIDTH[i::2])], F32)) for i in range(2)]
        s2 = c.enter_context(nc.psum_tensor("s2", [P, T], F32))
        tp = [c.enter_context(nc.psum_tensor(f"tp{i}", [P, 512], F32)) for i in range(2)]
        op = c.enter_context(nc.psum_tensor("op", [P, 512], F32))

        def group(i, c):
            if isinstance(i, int) and not 0 <= 2 * i + c < NSTEP:
                return None
            return Group(i * 2 + c, c % 2, i + c // 2)

        def at(i, c, s, delay):
            d, u = divmod(s - delay, NU)
            return group(i, c + d), u

        def due(i, c, s, slots):
            units = [(group(i, c - t // NU), u) for u, t in enumerate(slots) if t % NU == s]
            return sorted(((m, u) for m, u in units if m), key=lambda x: slots[x[1]], reverse=True)

        def span(m, u, k0=0, k1=None):
            return xe[m.p][:, START[u] + k0:START[u] + (WIDTH[u] if k1 is None else k1)]

        def plane(m, u, odd):
            return xe[m.p][:, START[u] + odd:START[u] + WIDTH[u]:2]

        def tail(u, shift):
            h = WIDTH[u] // 2
            return behind[:, u % NBEHIND, T // 2 - h + shift:T // 2 + shift]

        def scores(pe, dst, m, u):
            g, qb = UNITS[u]
            w = WIDTH[u]
            q = qs[m.p][g][:, qb * P:(qb + 1) * P]
            for lo in range(0, w, 512):
                hi = min(lo + 512, w)
                pe.matmul(dst[:, lo:hi], q, ks[m.p][g][:, lo:hi], start=True, stop=hi < w)
            return pe.matmul(dst[:, w - P:w], identb[:], maskb[:], start=False, stop=True)

        def pe_front(pe, m, u):
            if u % NB == 0:
                pe.wait_ge(sem(f"qk_loaded{UNITS[u][0]}{m.p}"), m.turn * 32 * NPART + 32 * NPART)
            if not first(m) or u >= 2:
                pe.wait_ge(sem("exp1"), m.n * NU + u - 1)
            scores(pe, s1[u % 2], m, u).then_inc(sem("scores1"), 1)

        def pe_back(pe, m, u):
            pe.wait_ge(sem("weighted"), m.n * NU + u + 1)
            scores(pe, s2, m, u).then_inc(sem("scores2"), 1)

        def pe_values(pe, m, k):
            u, j0, n = TILES[k]
            g, qb = UNITS[u]
            pe.wait_ge(sem("exp2"), m.n * NT + k + 1)
            if k == 0:
                pe.wait_ge(sem(f"v_loaded{m.p}"), m.turn * 16 + 16)
            if j0 == 0 and u % 4 == 0:
                pe.wait_ge(sem("ot"), m.n * NQ + u // 4 + 1)
            for i in range(n):
                j = j0 + i
                last = pe.matmul(op[32 * i:32 * i + VW, (u % 4) * P:(u % 4 + 1) * P],
                                 vals[m.p][:, j, g * VW:(g + 1) * VW], pt[k % NPT][:, i * P:(i + 1) * P],
                                 start=j0 == 0, stop=j + 4 > qb)
            last.then_inc(sem("products"), 1)

        def pe_transposes(pe, m, before, u):
            by_act = sum(ACT_SHIFT(v) for v in range(NU))
            before_u = sum(ACT_SHIFT(v) for v in range(u + 1))
            if ACT_SHIFT(u):
                pe.wait_ge(sem("act_shifted"), m.n * by_act + before_u)
            else:
                pe.wait_ge(sem("shifted"), m.n * (NU - by_act) + u + 1 - before_u)
            if u % 4 == 2 and (u > 2 or not first(m)):
                pe.wait_ge(sem("o"), m.n * NU + 4 * (u // 4) + 1)
            for k in tiles_of(u):
                _, j0, n = TILES[k]
                if not first(m) or k > 1:
                    pe.wait_ge(sem("exp2"), m.n * NT + k - 1)
                for i in range(n):
                    last = pe.transpose(tp[k % 2][:, i * P:(i + 1) * P], span(m, u, (j0 + i) * P, (j0 + i + 1) * P), ident[:])
                last.then_inc(sem("transposed"), 1)
                if k >= BEHIND:
                    pe_values(pe, m, k - BEHIND)
                elif before is not None:
                    pe_values(pe, before, k - BEHIND + NT)

        def pe_rows(pe, m, q, read):
            pe.wait_ge(sem("ot"), m.n * NQ + q + 1 + 1)
            pe.wait_ge(sem("exp2"), m.n * NT + read)
            for i in range(4):
                last = pe.transpose(tp[rows_bank(q)][:, i * P:(i + 1) * P], ot[q % 2][:, i * P:(i + 1) * P], ident[:])
            last.then_inc(sem("rows"), 1)

        def pe_step(pe, i, c):
            for s in range(NU):
                m, u = at(i, c, s, SUM)
                before, _ = at(i, c, s, SUM + NU)
                if m:
                    pe_transposes(pe, m, before, u)
                elif before and last(before) and u == 0:
                    for k in range(NT - BEHIND, NT):
                        pe_values(pe, before, k)
                back, v = at(i, c, s, SCORES2)
                if back:
                    pe_back(pe, back, v)
                front, v = at(i, c, s, 0)
                if front:
                    pe_front(pe, front, v)
                if m and u % 4 == 1 and u > 1:
                    pe_rows(pe, m, u // 4 - 1, tiles_of(u)[-1])
                elif before and u == 1:
                    pe_rows(pe, before, NQ - 1, NT + tiles_of(u)[-1] if m else NT)

        def act_step(act, i, c):
            for s in range(NU):
                m, u = at(i, c, s, EXP)
                if m:
                    act.wait_ge(sem("negmax"), m.n * NU + u + 1)
                    act.activation(span(m, u), s1[u % 2][:, 0:WIDTH[u]], ACT.Exp,
                                   bias=negmax[:, m.p, u:u + 1]).then_inc(sem("exp1"), 1)
                m, u = at(i, c, s, EXP2)
                if m:
                    for k in tiles_of(u):
                        n = TILES[k][2]
                        act.wait_ge(sem("transposed"), m.n * NT + k + 1)
                        if not first(m) or k >= NPT:
                            act.wait_ge(sem("products"), m.n * NT + k - NPT + 1)
                        act.activation(pt[k % NPT][:, 0:n * P], tp[k % 2][:, 0:n * P], ACT.Exp, scale=-1.0).then_inc(sem("exp2"), 1)
                if s == SQRT_SLOT and group(i, c - 1):
                    m = group(i, c - 1)
                    for g in range(G):
                        act.wait_ge(sem("clipped"), m.n * NU + NB * (g + 1))
                        act.activation(head(xe[m.p], g), head(xe[m.p], g), ACT.Sqrt).then_inc(sem("dist"), 1)
                m, u = at(i, c, s, EFFECT)
                if m and u % 2 == 0:
                    g = u // NB
                    act.wait_ge(sem("dist"), m.n * G + g + 1)
                    if u == 0:
                        act.wait_ge(sem(f"rate_loaded{m.p}"), m.turn * 16 + 16)
                    two = xe[m.p][:, START[u]:START[u + 1] + WIDTH[u + 1]]
                    act.activation(two, two, ACT.Exp, scale=rate[m.p][:, g:g + 1]).then_inc(sem("effect"), 1)
                m, u = at(i, c, s, WEIGH)
                if m and ACT_SHIFT(u):
                    act.wait_ge(sem("weighted"), m.n * NU + u + 1 + 1)
                    act.activation(span(m, u), span(m, u), ACT.Identity, scale=-1.0, bias=max2[:, m.p, u:u + 1]).then_inc(sem("act_shifted"), 1)

        def dve_copy_products(dve, m, q):
            dve.wait_ge(sem("products"), m.n * NT + tiles_of(4 * q + 3)[-1] + 1)
            dve.tensor_copy(ot[q % 2][:], op[:]).then_inc(sem("ot"), 1)

        def dve_rows(dve, m, q):
            dve.wait_ge(sem("rows"), m.n * NQ + q + 1)
            if q == 0:
                dve.wait_ge(sem("o_stored"), m.n * 16 + 1)
            for i in range(4):
                g, qb = UNITS[4 * q + i]
                dve.tensor_reduce(o[:, g, qb, :], tp[rows_bank(q)][:, i * P:(i + 1) * P].rearrange("p (j d) -> p d j", d=32)[:, 0:VW, 0:min(4, qb + 1)],
                                  AX.X, ALU.add).then_inc(sem("o"), 1)

        def dve_step(dve, i, c):
            for s in range(NU):
                m, u = at(i, c, s, SUM)
                before, _ = at(i, c, s, SUM + NU)
                if u == 1 and before:
                    dve_copy_products(dve, before, NQ - 1)
                elif u % 4 == 1 and u > 1 and m:
                    dve_copy_products(dve, m, u // 4 - 1)
                if u == 2 and before:
                    dve_rows(dve, before, NQ - 1)
                elif u % 4 == 2 and u > 2 and m:
                    dve_rows(dve, m, u // 4 - 1)
                m, u = at(i, c, s, WEIGH)
                if m:
                    dve.wait_ge(sem("effect"), m.n * (NU // 2) + u // 2 + 1)
                    dve.wait_ge(sem("scores2"), m.n * NU + u + 1)
                    alone(dve, sem)
                    dve.tensor_tensor_reduce(out=span(m, u), in0=span(m, u), in1=s2[:, 0:WIDTH[u]], scale=1.0, scalar=-3.4e38,
                                             op0=ALU.mult, op1=ALU.max, accum_out=max2[:, m.p, u:u + 1]).then_inc(sem("weighted"), 1)
                m, u = at(i, c, s, MAX)
                if m:
                    dve.wait_ge(sem("scores1"), m.n * NU + u + 1)
                    dve.tensor_reduce(negmax[:, m.p, u:u + 1], s1[u % 2][:, 0:WIDTH[u]], AX.X, ALU.max,
                                      negate=True).then_inc(sem("negmax"), 1)
                scanned = due(i, c, s, SCAN)
                for m, u in scanned:
                    dve.wait_ge(sem("exp1"), m.n * NU + u + 1)
                    dve.tensor_tensor_scan(tail(u, 0)[:, ::-1], plane(m, u, 1)[:, ::-1], plane(m, u, 0)[:, ::-1],
                                           0.0, ALU.add, ALU.add).then_inc(sem("scan"), 1)
                for m, u in due(i, c, s, CLIP):
                    if not POOL_ODD(u):
                        dve.wait_ge(sem("added"), m.n * NU + u + 1)
                        dve.tensor_tensor(plane(m, u, 1), tail(u, 1), pos[:, T - WIDTH[u] + 1:T:2], ALU.mult).then_inc(sem("far_odd"), 1)
                for m, u in scanned:
                    dve.wait_ge(sem("scan"), m.n * NU + u + 1)
                    dve.reciprocal(rtot[:, m.p, u:u + 1], tail(u, 0)[:, 0:1]).then_inc(sem("rtot"), 1)
                for m, u in due(i, c, s, CLIP):
                    if u == 0:
                        dve.wait_ge(sem(f"limit_loaded{m.p}"), m.turn * 16 + 16)
                    dve.wait_ge(sem("rtot"), m.n * NU + u + 1)
                    if not POOL_ODD(u):
                        dve.wait_ge(sem("far_odd"), m.n * NODD + sum(not POOL_ODD(v) for v in range(u + 1)))
                    dve.wait_ge(sem("far"), m.n * NU + u + 1)
                    dve.tensor_scalar(span(m, u), span(m, u), rtot[:, m.p, u:u + 1], limit[m.p][:, UNITS[u][0]:UNITS[u][0] + 1],
                                      ALU.mult, ALU.min).then_inc(sem("clipped"), 1)

        def pool_step(pool, i, c):
            for s in range(NU):
                m, u = at(i, c, s, WEIGH)
                if m and not ACT_SHIFT(u):
                    pool.wait_ge(sem("weighted"), m.n * NU + u + 1 + 1)
                    alone(pool, sem)
                    pool.tensor_scalar(span(m, u), span(m, u), -1.0, max2[:, m.p, u:u + 1], ALU.mult, ALU.add).then_inc(sem("shifted"), 1)
                for m, u in due(i, c, s, SCAN):
                    pool.wait_ge(sem("scan"), m.n * NU + u + 1)
                    pool.tensor_tensor(plane(m, u, 0), tail(u, 1), plane(m, u, 1), ALU.add).then_inc(sem("added"), 1)
                    pool.wait_ge(sem("added"), m.n * NU + u + 1)
                    if POOL_ODD(u):
                        pool.tensor_tensor(plane(m, u, 1), tail(u, 1), pos[:, T - WIDTH[u] + 1:T:2], ALU.mult)
                    pool.tensor_tensor(plane(m, u, 0), plane(m, u, 0), pos[:, T - WIDTH[u]:T:2], ALU.mult).then_inc(sem("far"), 1)

        def load_qk(sp, m, g):
            heads = st["qk"][DS((m.n * G + g) * DK, DK)].rearrange("d w r t -> w r d t")
            for r in range(NPART):
                to = slice(r * NPART * DK, (r + 1) * NPART * DK)
                sp.dma_start(qs[m.p][g][to, :], heads[0, r].unsqueeze(0).to_broadcast([NPART, DK, T])).then_inc(sem(f"qk_loaded{g}{m.p}"), 16)
                sp.dma_start(ks[m.p][g][to, :], heads[1]).then_inc(sem(f"qk_loaded{g}{m.p}"), 16)

        def load_limit(sp, m):
            sp.dma_start(limit[m.p][:], st["par"][DS(m.n, 1), 1].rearrange("a p g -> (a p) g")).then_inc(sem(f"limit_loaded{m.p}"), 16)

        def load_rate(sp, m):
            sp.dma_start(rate[m.p][:], st["par"][DS(m.n, 1), 0].rearrange("a p g -> (a p) g")).then_inc(sem(f"rate_loaded{m.p}"), 16)

        def load_values(sp, m):
            sp.dma_start(vals[m.p][:], st["v"][DS(m.n, 1)].rearrange("a p n w -> (a p) n w")).then_inc(sem(f"v_loaded{m.p}"), 16)

        def sp_step(sp, i, c):
            old, before, m, following = (group(i, c + d) for d in (-2, -1, 0, 1))
            if following and before:
                sp.wait_ge(sem("clipped"), before.n * NU + NU)
                alone(sp, sem)
                load_limit(sp, following)
            if old and m:
                sp.wait_ge(sem("scores2"), old.n * NU + NU)
                alone(sp, sem)
                load_qk(sp, m, 1)
                sp.wait_ge(sem("effect"), old.n * (NU // 2) + NU // 2)
                alone(sp, sem)
                load_rate(sp, m)
                sp.wait_ge(sem("products"), old.n * NT + NT)
                alone(sp, sem)
                load_values(sp, m)
            if old:
                sp.wait_ge(sem("o"), old.n * NU + NU + 1)
                alone(sp, sem)
                sp.dma_start(st["o"][DS(old.n, 1)].rearrange("a p w -> (a p) w"), o[:].rearrange("p g n d -> p (g n d)")).then_inc(sem("o_stored"), 16)
            if following and before:
                sp.wait_ge(sem("scores2"), before.n * NU + NB)
                alone(sp, sem)
                load_qk(sp, following, 0)

        def steps(eng, step):
            step(eng, 0, 0)
            step(eng, 0, 1)
            with eng.Fori(0, (NSTEP - 4) // 2) as i:
                step(eng, i, 2)
                step(eng, i, 3)
            for m in range(NSTEP - 2, NSTEP + 2):
                step(eng, m // 2, m % 2)

        with nc.Block() as block:
            @block.sync
            def _(sp):
                sp.sem_inc(sem("o_stored"), 1)
                sp.wait_ge(sem("pads"), 4 * G)
                for n in range(2):
                    m = group(0, n)
                    for g in range(G):
                        load_qk(sp, m, g)
                    load_limit(sp, m)
                    load_rate(sp, m)
                    load_values(sp, m)
                steps(sp, sp_step)
                sp.wait_ge(sem("o_stored"), 16 * NSTEP + 1)

            @block.gpsimd
            def _(pool):
                steps(pool, pool_step)

            @block.vector
            def _(dve):
                for p in range(2):
                    for g in range(G):
                        dve.memset(qs[p][g][D:KP, :], 0.0).then_inc(sem("pads"), 1)
                        dve.memset(ks[p][g][D:KP, :], 0.0).then_inc(sem("pads"), 1)
                dve.memset(op[:], 0.0).then_inc(sem("cleared"), 1)
                dve.memset(behind[:, :, T // 2:T // 2 + 1], 0.0).then_inc(sem("cleared"), 1)
                dve.sem_inc(sem("weighted"), 1)
                dve.sem_inc(sem("ot"), 1)
                dve.sem_inc(sem("o"), 1)
                steps(dve, dve_step)

            @block.scalar
            def _(act):
                steps(act, act_step)

            @block.tensor
            def _(pe):
                pe.wait_ge(sem("cleared"), 2)
                steps(pe, pe_step)


def channel_phase(nc, a, st, hold, out):
    ident = hold["ident"]
    with ExitStack() as c:
        sb = lambda n, s, d=F32: c.enter_context(nc.sbuf_tensor(n, s, d))
        names = {}

        def sem(n):
            if n not in names:
                names[n] = c.enter_context(nc.semaphore("c_" + n))
            return names[n]

        NC = E * HID // P
        ow, rw = sb("ow", [KP, D]), sb("rw", [KP, E])
        w1 = sb("w1", [KP, E * HID])
        w2 = sb("w2", [P, NC, D])
        b2 = sb("b2", [KP, D])
        expandf = sb("expandf", [KP, E * HID])
        expand = sb("expand", [KP, E * HID], BF16)
        prio = sb("prio", [P, E])
        rowmask = sb("rowmask", [P, 1])
        eps = sb("eps5", [P, 1])
        os_ = sb("os", [P, H, NB, VW])
        rden = sb("rden", [P, H, NB])
        att = sb("att", [P, NB, H, DK])
        aT = sb("aT", [KP, T])
        h1 = sb("h1c", [P, NB, D])
        res = sb("res", [P, NB, D])
        xc, sq = sb("xc2", [P, NB, D]), sb("sq2", [P, NB, D])
        stat = sb("stat2", [P, 4, NB])
        h2 = sb("h2", [P, NB, D])
        h2T = sb("h2T", [KP, T])
        best = sb("best", [P, 2, NB])
        hot = sb("hot", [P, NB, E])
        rank = sb("rank", [P, NB, E])
        hotT = sb("hotT", [KP, T])
        coldT = sb("coldT", [KP, T], BF16)
        hid = sb("hid", [P, 2, T])
        fT = sb("fT", [D, T])
        y = sb("y", [P, NB, D])
        q0, q1, q2, q3 = (c.enter_context(nc.psum_tensor(f"pc{i}", [P, T], F32)) for i in range(4))
        half = lambda t, i: t[:, i * 512:(i + 1) * 512]
        blk = lambda t, i, w=P: t[:, i * w:(i + 1) * w]
        rows = lambda t: t.rearrange("p (n d) -> p n d", d=D)

        def norm_first(dve, x, n):
            dve.tensor_reduce(stat[:, 0, :], x, AX.X, ALU.add).then_inc(sem("ln"), 1)
            dve.wait_ge(sem("ln"), n + 1)
            dve.tensor_scalar(stat[:, 1, :], stat[:, 0, :], -1.0 / D, None, ALU.mult).then_inc(sem("ln"), 1)
            dve.wait_ge(sem("ln"), n + 2)
            dve.tensor_tensor(xc[:], x, stat[:, 1, :].unsqueeze(2).to_broadcast([P, NB, D]), ALU.add).then_inc(sem("ln"), 1)
            dve.wait_ge(sem("ln"), n + 3)
            dve.tensor_tensor(sq[:], xc[:], xc[:], ALU.mult).then_inc(sem("ln"), 1)
            dve.wait_ge(sem("ln"), n + 4)
            dve.tensor_reduce(stat[:, 2, :], sq[:], AX.X, ALU.add).then_inc(sem("var"), 1)

        def norm_second(dve, to, n, nstd, done):
            dve.wait_ge(sem("std"), nstd)
            dve.reciprocal(stat[:, 1, :], stat[:, 3, :]).then_inc(sem("ln"), 1)
            dve.wait_ge(sem("ln"), n + 5)
            dve.tensor_tensor(to, xc[:], stat[:, 1, :].unsqueeze(2).to_broadcast([P, NB, D]), ALU.mult).then_inc(done, 1)

        with nc.Block() as block:
            @block.sync
            def _(sp):
                for t, n in ((ow, "ow"), (rw, "rw"), (w1, "w1"), (w2, "w2"), (b2, "b2"), (expandf, "c_expand"),
                             (prio, "c_prio"), (rowmask, "c_rowmask"), (eps, "c_eps5")):
                    sp.dma_start(t[:], a[n]).then_inc(sem("weights"), 16)
                sp.sem_inc(sem("stored"), 1)
                with sp.Fori(0, B) as b:
                    sp.wait_ge(sem("att"), b + 1)
                    sp.dma_start(os_[:].rearrange("p (s g) n d -> p s (g n d)", g=G),
                                 st["o"][DS(b * HP, HP)].rearrange("s p w -> p s w")).then_inc(sem("o_loaded"), 16)
                    sp.wait_ge(sem("res"), b + 1)
                    sp.dma_start(h1[:], st["h1"][DS(b, 1)].rearrange("a p n d -> (a p) n d")).then_inc(sem("h1_loaded"), 16)
                    sp.wait_ge(sem("y"), b + 1)
                    sp.dma_start(out[DS(b, 1)].rearrange("a (n p) d -> (a p) n d", p=P), y[:]).then_inc(sem("stored"), 16)
                sp.wait_ge(sem("stored"), 16 * B + 1)

            @block.vector
            def _(dve):
                for t in (aT, h2T):
                    dve.memset(t[D:KP, :], 0.0).then_inc(sem("pads"), 1)
                dve.memset(hotT[:], 0.0).then_inc(sem("pads"), 1)
                dve.memset(coldT[:], 0.0).then_inc(sem("pads"), 1)
                dve.wait_ge(sem("pads"), 4)
                dve.memset(aT[D:D + 1, :], 1.0).then_inc(sem("pads"), 1)
                dve.memset(h2T[D:D + 1, :], 1.0).then_inc(sem("pads"), 1)
                dve.wait_ge(sem("weights"), 16 * 9)
                dve.tensor_copy(expand[:], expandf[:]).then_inc(sem("expand"), 1)
                dve.sem_inc(sem("att"), 1)
                dve.sem_inc(sem("res"), 1)
                dve.sem_inc(sem("res2"), 1)
                dve.wait_ge(sem("pads"), 6)
                with dve.Fori(0, B) as b:
                    dve.wait_ge(sem("o_loaded"), 16 * b + 16)
                    dve.reciprocal(rden[:], os_[:, :, :, DK]).then_inc(sem("rden"), 1)
                    dve.wait_ge(sem("rden"), 2 * b + 1)
                    dve.tensor_scalar(rden[:, :, 0], rden[:, :, 0], rowmask[:, 0:1], None, ALU.mult).then_inc(sem("rden"), 1)
                    dve.wait_ge(sem("rden"), 2 * b + 2)
                    dve.tensor_tensor(att[:].rearrange("p n h d -> p h n d"), os_[:, :, :, 0:DK],
                                      rden[:].unsqueeze(3).to_broadcast([P, H, NB, DK]), ALU.mult).then_inc(sem("att"), 1)
                    dve.wait_ge(sem("attended"), b + 1)
                    dve.wait_ge(sem("h1_loaded"), 16 * b + 16)
                    dve.tensor_tensor(res[:], rows(q1[:, 0:512]), h1[:], ALU.add).then_inc(sem("res"), 1)
                    dve.wait_ge(sem("res"), b + 1 + 1)
                    norm_first(dve, res[:], 10 * b)
                    norm_second(dve, h2[:], 10 * b, 2 * b + 1, sem("h2"))
                    dve.wait_ge(sem("logits"), b + 1)
                    logits = q1[:, 512:512 + NB * E].rearrange("p (n e) -> p n e", e=E)
                    dve.tensor_reduce(best[:, 0, :], logits, AX.X, ALU.max).then_inc(sem("hot"), 1)
                    dve.wait_ge(sem("hot"), 5 * b + 1)
                    dve.tensor_tensor(rank[:], logits, best[:, 0, :].unsqueeze(2).to_broadcast([P, NB, E]), ALU.is_ge).then_inc(sem("hot"), 1)
                    dve.wait_ge(sem("hot"), 5 * b + 2)
                    dve.tensor_tensor(rank[:], rank[:], prio[:].unsqueeze(1).to_broadcast([P, NB, E]), ALU.mult).then_inc(sem("hot"), 1)
                    dve.wait_ge(sem("hot"), 5 * b + 3)
                    dve.tensor_reduce(best[:, 1, :], rank[:], AX.X, ALU.max).then_inc(sem("hot"), 1)
                    dve.wait_ge(sem("hot"), 5 * b + 4)
                    dve.tensor_tensor(hot[:], rank[:], best[:, 1, :].unsqueeze(2).to_broadcast([P, NB, E]), ALU.is_equal).then_inc(sem("hot"), 1)
                    dve.wait_ge(sem("hotT_ps"), b + 1)
                    dve.tensor_copy(hotT[0:E, :], q2[0:E, :]).then_inc(sem("hotT"), 1)
                    dve.wait_ge(sem("hotT"), b + 1)
                    dve.tensor_scalar(coldT[0:E, :], hotT[0:E, :], -1.0, None, ALU.add).then_inc(sem("coldT"), 1)
                    dve.wait_ge(sem("experts"), b + 1)
                    dve.tensor_tensor(res[:], rows(q1[:, 0:512]), h2[:], ALU.add).then_inc(sem("res2"), 1)
                    dve.wait_ge(sem("res2"), b + 1 + 1)
                    norm_first(dve, res[:], 10 * b + 5)
                    dve.wait_ge(sem("stored"), 16 * b + 1)
                    norm_second(dve, y[:], 10 * b + 5, 2 * b + 2, sem("y"))

            @block.scalar
            def _(act):
                act.wait_ge(sem("weights"), 16 * 9)
                act.wait_ge(sem("pads"), 6)
                with act.Fori(0, B) as b:
                    act.wait_ge(sem("aT_ps"), b + 1)
                    act.copy(aT[0:D, :], q0[0:D, :]).then_inc(sem("aT"), 1)
                    act.wait_ge(sem("var"), 2 * b + 1)
                    act.activation(stat[:, 3, :], stat[:, 2, :], ACT.Sqrt, scale=1.0 / D, bias=eps[:, 0:1]).then_inc(sem("std"), 1)
                    act.wait_ge(sem("h2T_ps"), b + 1)
                    act.copy(h2T[0:D, :], q0[0:D, :]).then_inc(sem("h2T"), 1)
                    for i in range(NC):
                        act.wait_ge(sem("hidden"), NC * b + i + 1)
                        if i >= 2:
                            act.wait_ge(sem("mixed"), NC * b + i - 1)
                        act.activation(hid[:, i % 2, :], (q3, q0)[i % 2][:], ACT.Relu).then_inc(sem("relu"), 1)
                    act.wait_ge(sem("mixed"), NC * b + NC)
                    act.activation(fT[:], q2[0:D, :], ACT.Relu).then_inc(sem("fT"), 1)
                    act.wait_ge(sem("var"), 2 * b + 2)
                    act.activation(stat[:, 3, :], stat[:, 2, :], ACT.Sqrt, scale=1.0 / D, bias=eps[:, 0:1]).then_inc(sem("std"), 1)

            @block.tensor
            def _(pe):
                mm = pe.matmul
                pe.wait_ge(sem("weights"), 16 * 9)
                pe.wait_ge(sem("pads"), 6)
                pe.wait_ge(sem("expand"), 1)
                with pe.Fori(0, B) as b:
                    pe.wait_ge(sem("att"), b + 1 + 1)
                    alone(pe, sem)
                    for n in range(NB):
                        last = pe.transpose(blk(q0, n)[0:D, :], att[:, n].rearrange("p h d -> p (h d)"), ident[:])
                    last.then_inc(sem("aT_ps"), 1)
                    pe.wait_ge(sem("aT"), b + 1)
                    pe.wait_ge(sem("res2"), b + 1)
                    for n in range(NB):
                        last = mm(blk(q1, n, D), blk(aT, n), ow[:], start=True, stop=True)
                    last.then_inc(sem("attended"), 1)
                    pe.wait_ge(sem("h2"), b + 1)
                    alone(pe, sem)
                    for n in range(NB):
                        last = pe.transpose(blk(q0, n)[0:D, :], h2[:, n, :], ident[:])
                    last.then_inc(sem("h2T_ps"), 1)
                    pe.wait_ge(sem("h2T"), b + 1)
                    for n in range(NB):
                        last = mm(q1[:, 512 + n * E:512 + (n + 1) * E], blk(h2T, n), rw[:], start=True, stop=True)
                    last.then_inc(sem("logits"), 1)
                    pe.wait_ge(sem("hot"), 5 * b + 5)
                    alone(pe, sem)
                    for n in range(NB):
                        last = pe.transpose(blk(q2, n)[0:E, :], hot[:, n, :], ident[:])
                    last.then_inc(sem("hotT_ps"), 1)
                    pe.wait_ge(sem("coldT"), b + 1)
                    for i in range(NC + 1):
                        if i < NC:
                            if i >= 2:
                                pe.wait_ge(sem("relu"), NC * b + i - 1)
                            for n in range(2):
                                dst = half((q3, q0)[i % 2], n)
                                mm(dst, blk(w1, i), half(h2T, n), start=True, stop=False)
                                last = mm(dst, blk(expand, i), half(coldT, n), start=False, stop=True)
                            last.then_inc(sem("hidden"), 1)
                        if i == 1:
                            pe.wait_ge(sem("hotT"), b + 1)
                            for n in range(2):
                                mm(half(q2, n)[0:D, :], b2[:], half(hotT, n), start=True, stop=False)
                        if i >= 1:
                            pe.wait_ge(sem("relu"), NC * b + i)
                            for n in range(2):
                                last = mm(half(q2, n)[0:D, :], w2[:, i - 1, :], hid[:, (i - 1) % 2, n * 512:(n + 1) * 512],
                                          start=False, stop=i == NC)
                            last.then_inc(sem("mixed"), 1)
                    pe.wait_ge(sem("fT"), b + 1)
                    alone(pe, sem)
                    for n in range(NB):
                        last = pe.transpose(blk(q1, n, D), fT[:, blk_of(n)], ident[0:D, 0:D])
                    last.then_inc(sem("experts"), 1)


def blk_of(n):
    return slice(n * P, (n + 1) * P)


def program(nc, a, out):
    st = {
        "par": nc.dram_tensor("step_par", [NSTEP, 2, P, G], F32).ap(),
        "h1": nc.dram_tensor("tok_rows", [B, P, NB, D], F32).ap(),
        "v": nc.dram_tensor("value_rows", [NSTEP, P, NB, G * VW], F32).ap(),
        "qk": nc.dram_tensor("qk_parts", [B * H * DK, 2, NPART, T], BF16).ap(),
        "o": nc.dram_tensor("attended_rows", [NSTEP, P, G * NB * VW], F32).ap(),
    }
    with ExitStack() as c:
        hold = {
            "ident": c.enter_context(nc.sbuf_tensor("ident", [P, P], F32)),
            "identb": c.enter_context(nc.sbuf_tensor("identb", [P, P], BF16)),
            "maskb": c.enter_context(nc.sbuf_tensor("maskb", [P, P], BF16)),
            "pos": c.enter_context(nc.sbuf_tensor("pos", [P, T], F32)),
            "gam": c.enter_context(nc.sbuf_tensor("gam", [P, H], F32)),
        }
        setup_phase(nc, a, st, hold)
        token_phase(nc, a, st, hold)
        attention_phase(nc, a, st, hold)
        channel_phase(nc, a, st, hold, out)


def kernel(**inputs):
    import numpy as np
    import concourse.bacc as bacc
    from concourse.bass_utils import run_bass_kernel_spmd

    f = np.float32
    i = {n: np.asarray(x) for n, x in inputs.items()}
    tok, att, ffn = ({n[len(k):]: x for n, x in i.items() if n.startswith(k)} for k in ("L0_tok_", "L0_attn_", "L0_ffn_"))

    def padded(rows, *parts):
        parts = [p.reshape(-1, p.shape[-1]) for p in parts]
        return np.concatenate(parts + [np.zeros((rows - sum(len(p) for p in parts), parts[0].shape[1]), f)], 0)

    wva = np.zeros((D + 1, H, VW), f)
    wva[:D, :, :DK] = att["v_w"].T.reshape(D, H, DK)
    wva[D, :, :DK] = att["v_b"].reshape(H, DK)
    wva[D, :, DK] = 1.0
    taps = att["conv_w"].transpose(2, 1, 0)
    cw = np.zeros((P, 3, D), f)
    for k in range(TAPS):
        cw[D * (k % 2):D * (k % 2) + D, k // 2] = taps[k]
    r, x = np.arange(P)[:, None], np.arange(T)[None, :]
    arrays = {
        "xT": i["x"].reshape(B, T, D).transpose(0, 2, 1),
        "gammaT": tok["d_gamma_batched"].T.reshape(NB, P, T).transpose(1, 0, 2),
        "wq": padded(KP, tok["Wq"], tok["bq"]), "wk": padded(KP, tok["Wk"], tok["bk"]), "wv": padded(KP, tok["Wv"], tok["bv"]),
        "wo2": np.concatenate([tok["Wo"], tok["Wo"]], 0),
        "bo_row": padded(KP, np.tile(tok["bo"], NB)),
        "cb_row": padded(KP, np.tile(att["conv_b"], NB)),
        "beta": np.repeat(att["sqrt_beta"].reshape(1, D), P, 0),
        "conv_w": cw,
        "prelu": np.repeat(tok["prelu_a"].reshape(1, 1), P, 0),
        "ln_wb": np.stack([att["ln_w"], att["ln_b"]], 1),
        "wqk": padded(KP, np.concatenate([att["q_w"].T, att["k_w"].T], 1), np.concatenate([att["q_b"], att["k_b"]])),
        "wva": padded(KP, wva.reshape(D + 1, H * VW)),
        "gammas": np.repeat(att["gammas"].reshape(1, H), P, 0),
        "ow": padded(KP, att["out_w"].T, att["out_b"]),
        "rw": padded(KP, ffn["router_w"].T, ffn["router_b"]),
        "w1": padded(KP, ffn["W1"].transpose(1, 0, 2).reshape(D, E * HID), ffn["b1"].reshape(1, E * HID)),
        "w2": ffn["W2"].reshape(E * HID // P, P, D).transpose(1, 0, 2),
        "b2": padded(KP, ffn["b2"]),
        "c_ident": np.eye(P, dtype=f),
        "c_mask": np.where(np.arange(P)[None, :] > r, f(MASKED), f(0)).astype(f),
        "c_pos": np.maximum(r + T - P - x, 0).astype(f),
        "c_ones_row": padded(KP, np.ones((1, P), f)),
        "c_eps12": np.full((P, 1), 1e-12, f), "c_eps5": np.full((P, 1), 1e-5, f),
        "c_qk_scale": np.concatenate([np.full((D, 1), DK ** -0.5, f), np.ones((D, 1), f)], 0),
        "c_expand": padded(KP, np.repeat(np.eye(E, dtype=f), HID, 1) * f(1e30)),
        "c_prio": np.repeat(np.arange(E, 0, -1, dtype=f)[None], P, 0),
        "c_rowmask": (r > 0).astype(f),
    }
    nc = bacc.Bacc("TRN2", target_bir_lowering=False, num_devices=1)
    arrays = {n: np.ascontiguousarray(x) for n, x in arrays.items()}
    a = {n: nc.dram_tensor("in_" + n, x.shape, mybir.dt.from_np(x.dtype), kind="ExternalInput").ap() for n, x in arrays.items()}
    out = nc.dram_tensor("out_rows", (B, T, D), F32, kind="ExternalOutput").ap()
    program(nc, a, out)
    got = run_bass_kernel_spmd(nc, [{"in_" + n: x for n, x in arrays.items()}], core_ids=[0])
    return got.results[0]["out_rows"]
```

```python
import math
from collections import namedtuple
from contextlib import ExitStack

import concourse.bass as bass
from concourse import mybir

ALU = mybir.AluOpType
ACT = mybir.ActivationFunctionType
AX = mybir.AxisListType
F32 = mybir.dt.float32
BF16 = mybir.dt.bfloat16
DS = bass.ds

P = 128
B, T, D = 16, 1024, 64
NB = T // P
H, DK = 8, 8
TAPS = 5
E, HID = 32, 16
KP = 96
NPART = 3
VW = DK + 1

G = 2
HP = H // G
NSTEP = B * HP
ORDER = (7, 0, 6, 1, 5, 2, 4, 3)
UNITS = [(g, qb) for g in range(G) for qb in ORDER]
NU = len(UNITS)
HEADW = sum(P * (qb + 1) for qb in range(NB))
WIDTH = [P * (qb + 1) for g, qb in UNITS]
START = [sum(WIDTH[:u]) for u in range(NU)]
TILES = [(u, j, min(4, qb + 1 - j)) for u, (g, qb) in enumerate(UNITS) for j in range(0, qb + 1, 4)]
NT = len(TILES)
NQ = NU // 4
MAX, EXP = 1, 2
SQRT_SLOT = 6
EFFECT = NU + SQRT_SLOT
SCORES2 = EFFECT + 1
WEIGH = SCORES2 + 1
SUM = WEIGH + 1
EXP2 = SUM + 1
TILES_BEHIND = 2
NPT = 3
NBEHIND = 8
NHELD = 5
HELD = range(SQRT_SLOT - 1 - NHELD, SQRT_SLOT - 1)
SCAN = [SQRT_SLOT + 1 if u in HELD else u + 3 for u in range(NU)]
CLIP = [SQRT_SLOT + 1 + (u - HELD[0]) // 2 if u in HELD else u + 5 for u in range(NU)]
MASKED = -1e32
LN_FLOOR = math.log(1e-5)

Group = namedtuple("Group", "n p turn")


def pool_takes_odd(u):
    return u % 2 == 0


def act_shifts(u):
    return u % 4 == 0


def up_to(u, who):
    return sum(who(v) for v in range(u + 1))


def first(m):
    return isinstance(m.n, int) and m.n == 0


def last(m):
    return isinstance(m.n, int) and m.n == NSTEP - 1


def tiles_of(u):
    return [k for k, tile in enumerate(TILES) if tile[0] == u]


def rows_bank(q):
    return (tiles_of((4 * q + 5) % NU)[-1] + 1) % 2


def head(t, g):
    return t[:, g * HEADW:(g + 1) * HEADW]


def alone(eng, sem):
    eng.sem_inc(sem("passed"), 1)


def setup_phase(nc, a, st, hold):
    ident, identb, maskb, pos, gam = hold["ident"], hold["identb"], hold["maskb"], hold["pos"], hold["gam"]
    with ExitStack() as c:
        sb = lambda n, s, d=F32: c.enter_context(nc.sbuf_tensor(n, s, d))
        sem = lambda n: c.enter_context(nc.semaphore(n))
        maskf = sb("maskf", [P, P])
        e = sb("gam_exp", [P, 4, H])
        par = sb("par", [P, 2, H])
        loaded, ab, ex, ln, sp, stored, rc = (sem("set_" + n) for n in
                                              ("loaded", "abs", "exp", "ln", "sp", "stored", "rc"))
        conv = sem("set_conv")
        with nc.Block() as block:
            @block.sync
            def _(sp_):
                sp_.dma_start(ident[:], a["c_ident"]).then_inc(loaded, 16)
                sp_.dma_start(maskf[:], a["c_mask"]).then_inc(loaded, 16)
                sp_.dma_start(pos[:], a["c_pos"]).then_inc(loaded, 16)
                sp_.dma_start(gam[:], a["gammas"]).then_inc(loaded, 16)
                sp_.wait_ge(sp, 4)
                with sp_.Fori(0, B) as b:
                    for s in range(HP):
                        for k in range(2):
                            sp_.dma_start(st["par"][DS(b * HP + s, 1), k].rearrange("a p g -> (a p) g"),
                                          par[:, k, s * G:(s + 1) * G]).then_inc(stored, 16)
                sp_.wait_ge(stored, 16 * 2 * NSTEP)

            @block.vector
            def _(dve):
                dve.wait_ge(loaded, 64)
                dve.tensor_copy(identb[:], ident[:]).then_inc(conv, 1)
                dve.tensor_copy(maskb[:], maskf[:]).then_inc(conv, 1)
                dve.scalar_tensor_tensor(e[:, 0], gam[:], -1.0, gam[:], ALU.mult, ALU.max).then_inc(ab, 1)
                dve.wait_ge(ln, 1)
                dve.scalar_tensor_tensor(e[:, 3], gam[:], 0.0, e[:, 2], ALU.max, ALU.add).then_inc(sp, 1)
                dve.wait_ge(sp, 1)
                dve.tensor_scalar(par[:, 0], e[:, 3], -1.0, None, ALU.mult).then_inc(sp, 1)
                dve.reciprocal(e[:, 0], e[:, 3]).then_inc(sp, 1)
                dve.wait_ge(sp, 3)
                dve.scalar_tensor_tensor(par[:, 1], e[:, 0], LN_FLOOR ** 2, e[:, 0], ALU.mult, ALU.mult).then_inc(sp, 1)

            @block.scalar
            def _(act):
                act.wait_ge(ab, 1)
                act.activation(e[:, 1], e[:, 0], ACT.Exp, scale=-1.0).then_inc(ex, 1)
                act.wait_ge(ex, 1)
                act.activation(e[:, 2], e[:, 1], ACT.Ln, bias=1.0).then_inc(ln, 1)


def token_phase(nc, a, st, hold):
    ident = hold["ident"]
    with ExitStack() as c:
        sb = lambda n, s, d=F32: c.enter_context(nc.sbuf_tensor(n, s, d))
        names = {}

        def sem(n):
            if n not in names:
                names[n] = c.enter_context(nc.semaphore("a_" + n))
            return names[n]

        gammaT = sb("gammaT", [P, NB, T])
        xT = sb("xT", [KP, T])
        wq, wk, wv = sb("wq", [KP, D]), sb("wk", [KP, D]), sb("wv", [KP, D])
        wo2 = sb("wo2", [P, D])
        bo_row, cb_row, ones_row = sb("bo_row", [KP, NB * D]), sb("cb_row", [KP, NB * D]), sb("ones_row", [KP, P])
        beta = sb("beta", [P, D])
        beta2 = sb("beta2", [P, 2, D])
        cw = sb("cw", [P, 3, D])
        prelu = sb("prelu", [P, 1])
        eps = sb("eps", [P, 1])
        ln_wb = sb("ln_wb", [D, 2])
        wqk = sb("wqk", [KP, 2 * D])
        wva = sb("wva", [KP, H * VW])
        qk_scale = sb("qk_scale", [P, 1])
        qT, kT = sb("qT", [KP, T]), sb("kT", [KP, T])
        v = sb("v", [P, NB, D])
        gm = sb("gm", [P, 2, T])
        retT = sb("retT", [P, T])
        neg = sb("neg", [P, NB, D])
        h1 = sb("h1", [P, NB, 2, D])
        hT = sb("hT", [P, T + 4])
        stat = sb("stat", [P, 4, NB])
        xc, sq = sb("xc", [P, NB, D]), sb("sq", [P, NB, D])
        nT = sb("nT", [KP, T])
        qk = sb("qk", [P, T])
        rest = sb("rest", [P, T])
        part = sb("part", [P, NPART, T], BF16)
        va = sb("va", [P, NB, H * VW])
        sc = [c.enter_context(nc.psum_tensor(f"a_scores{i}", [P, T], F32)) for i in range(2)]
        ret = c.enter_context(nc.psum_tensor("a_ret", [P, T], F32))
        vy = c.enter_context(nc.psum_tensor("a_vy", [P, NB * D], F32))
        piece = c.enter_context(nc.psum_tensor("a_piece", [P, T // 2], F32))
        TH, NH = T // 2, NB // 2
        half = lambda t, i: t[:, i * TH:(i + 1) * TH]
        blk = lambda t, i, w=P: t[:, i * w:(i + 1) * w]
        rows = lambda t: t[:].rearrange("p (n d) -> p n d", d=D)

        def steps(eng, step):
            step(eng, 0, None)
            with eng.Fori(0, B - 1) as i:
                step(eng, i + 1, i)
            step(eng, None, B - 1)

        def load_x(sp, b):
            sp.wait_ge(sem("v_proj"), b + 1)
            sp.dma_start(xT[0:D, :], a["xT"][DS(b, 1)].rearrange("a d t -> (a d) t")).then_inc(sem("x_loaded"), 16)

        def store_h1(sp, b):
            sp.wait_ge(sem("h1"), b + 1)
            sp.dma_start(st["h1"][DS(b, 1)].rearrange("a p n d -> (a p) n d"), h1[:, :, 0, :]).then_inc(sem("h1_stored"), 16)

        def store_qkv(sp, e):
            sp.wait_ge(sem("va"), e * 2 + 2 + 1)
            for s in range(HP):
                sp.dma_start(st["v"][DS(e * HP + s, 1)].rearrange("a p n w -> (a p) n w"),
                             va[:, :, s * G * VW:(s + 1) * G * VW]).then_inc(sem("v_stored"), 16)
            sp.wait_ge(sem("part2"), e + 1)
            for r in range(NPART):
                for w in range(2):
                    sp.dma_start(st["qk"][DS(e * D, D), w, r], part[w * D:(w + 1) * D, r, :]).then_inc(sem("qk_stored"), 16)

        def pool_step(pool, b, e):
            if e is not None:
                pool.wait_ge(sem("part0"), e * 2 + 2)
                pool.tensor_tensor(rest[:], qk[:], part[:, 0, :], ALU.subtract).then_inc(sem("rest"), 1)
            if b is not None:
                pool.wait_ge(sem("h1"), b + 1)
                alone(pool, sem)
                pool.tensor_copy(h1[:, :, 1, :], h1[:, :, 0, :]).then_inc(sem("h1_twice"), 1)

        def dve_gate(dve, b, s):
            dve.wait_ge(sem("scores"), b * NB + s + 1)
            if s >= 2:
                dve.wait_ge(sem("ret"), b * NB + s - 1)
            dve.tensor_tensor(gm[:, s % 2, :], sc[s % 2][:], gammaT[:, s, :], ALU.mult).then_inc(sem("gated"), 1)

        def dve_h1_rows(dve, e, h):
            dve.wait_ge(sem("h1T"), e * 2 + h + 1)
            dve.tensor_copy(hT[D:P, 3 + h * TH:3 + (h + 1) * TH], piece[D:P, :]).then_inc(sem("hT_high"), 1)

        def dve_centre(dve, e):
            dve.wait_ge(sem("z"), e + 1)
            dve.tensor_reduce(stat[:, 0, :], rows(piece), AX.X, ALU.add).then_inc(sem("ln"), 1)
            dve.wait_ge(sem("ln"), e * 6 + 1)
            dve.tensor_scalar(stat[:, 1, :], stat[:, 0, :], -1.0 / D, None, ALU.mult).then_inc(sem("ln"), 1)
            dve.wait_ge(sem("ln"), e * 6 + 2)
            dve.tensor_tensor(xc[:], rows(piece), stat[:, 1, :].unsqueeze(2).to_broadcast([P, NB, D]), ALU.add).then_inc(sem("ln"), 1)
            dve.wait_ge(sem("ln"), e * 6 + 3)
            dve.tensor_tensor(sq[:], xc[:], xc[:], ALU.mult).then_inc(sem("ln"), 1)
            dve.wait_ge(sem("ln"), e * 6 + 4)
            dve.tensor_reduce(stat[:, 2, :], sq[:], AX.X, ALU.add).then_inc(sem("var"), 1)

        def dve_scale(dve, e):
            dve.wait_ge(sem("std"), e + 1)
            dve.reciprocal(stat[:, 1, :], stat[:, 3, :]).then_inc(sem("ln"), 1)
            dve.wait_ge(sem("ln"), e * 6 + 5)
            dve.tensor_tensor(xc[:], xc[:], stat[:, 1, :].unsqueeze(2).to_broadcast([P, NB, D]), ALU.mult).then_inc(sem("ln"), 1)

        def dve_step(dve, b, e):
            if b is not None:
                dve.wait_ge(sem("qk_proj"), b * 2 + 2)
                dve.tensor_copy(kT[0:D, :], sc[1][0:D, :]).then_inc(sem("kT"), 1)
            for s in range(NB):
                if b is not None:
                    dve_gate(dve, b, s)
                if e is not None:
                    if s < 2:
                        dve_h1_rows(dve, e, s)
                    elif s == 2:
                        dve_centre(dve, e)
                    elif s == 3:
                        dve_scale(dve, e)
            if b is not None:
                dve.wait_ge(sem("y"), b + 1)
                dve.tensor_scalar(neg[:], rows(vy), 0.0, prelu[:, 0:1], ALU.min, ALU.mult).then_inc(sem("neg"), 1)
                dve.wait_ge(sem("neg"), b + 1)
                dve.wait_ge(sem("h1_stored"), b * 16 + 1)
                if e is not None:
                    dve.wait_ge(sem("h1T"), e * 2 + 2)
                dve.scalar_tensor_tensor(h1[:, :, 0, :], rows(vy), 0.0, neg[:], ALU.max, ALU.add).then_inc(sem("h1"), 1)
            if e is not None:
                dve.wait_ge(sem("rest"), e + 1)
                dve.tensor_copy(part[:, 1, :], rest[:]).then_inc(sem("part1"), 1)
                dve.wait_ge(sem("part1"), e + 1)
                dve.tensor_tensor(part[:, 2, :], rest[:], part[:, 1, :], ALU.subtract).then_inc(sem("part2"), 1)

        def act_step(act, b, e):
            if b is not None:
                act.wait_ge(sem("qk_proj"), b * 2 + 1)
                act.copy(qT[0:D, :], sc[0][0:D, :]).then_inc(sem("qT"), 1)
                act.wait_ge(sem("v_proj"), b + 1 + 1)
                act.copy(v[:].rearrange("p n d -> p (n d)"), vy[:]).then_inc(sem("v"), 1)
            if e is not None:
                for h in range(2):
                    act.wait_ge(sem("h1T"), e * 2 + h + 1)
                    act.copy(hT[0:D, 4 + h * TH:4 + (h + 1) * TH], piece[0:D, :]).then_inc(sem("hT_low"), 1)
                act.wait_ge(sem("var"), e + 1)
                act.activation(stat[:, 3, :], stat[:, 2, :], ACT.Sqrt, scale=1.0 / D, bias=eps[:, 0:1]).then_inc(sem("std"), 1)
                for h in range(2):
                    act.wait_ge(sem("nT_ps"), e * 2 + h + 1)
                    act.activation(half(nT, h)[0:D, :], piece[0:D, :], ACT.Identity, scale=ln_wb[:, 0:1], bias=ln_wb[:, 1:2]).then_inc(sem("nT"), 1)
                act.wait_ge(sem("qk_stored"), e * (16 * 2 * NPART) + 1)
                for h in range(2):
                    act.wait_ge(sem("qk2"), e * 2 + h + 1)
                    act.activation(half(part[:, 0, :], h), piece[:], ACT.Copy, scale=qk_scale[:, 0:1])
                    act.activation(half(qk, h), piece[:], ACT.Copy, scale=qk_scale[:, 0:1]).then_inc(sem("part0"), 1)
            if b is not None:
                act.wait_ge(sem("ret"), b * NB + NB)
                act.copy(retT[:], ret[:]).then_inc(sem("retT"), 1)
            if e is not None:
                act.wait_ge(sem("v_stored"), e * (16 * HP) + 1)
                for h in range(2):
                    act.wait_ge(sem("va_ps"), e * 2 + h + 1)
                    act.copy(va[:, h * NH:(h + 1) * NH, :], piece[:, 0:NH * P].rearrange("p (n w) -> p n w", w=P)[:, :, 0:H * VW]).then_inc(sem("va"), 1)

        def pe_project(pe, b):
            pe.wait_ge(sem("x_loaded"), b * 16 + 16)
            if not isinstance(b, int):
                pe.wait_ge(sem("gated"), b * NB)
            for w, p in zip((wq, wk), sc):
                for n in range(2):
                    last = pe.matmul(half(p, n)[0:D, :], w[:], half(xT, n), start=True, stop=True)
                last.then_inc(sem("qk_proj"), 1)
            if not isinstance(b, int):
                pe.wait_ge(sem("h1"), b)
            for n in range(NB):
                last = pe.matmul(blk(vy, n, D), blk(xT, n), wv[:], start=True, stop=True)
            last.then_inc(sem("v_proj"), 1)
            pe.wait_ge(sem("qT"), b + 1)
            pe.wait_ge(sem("kT"), b + 1)

        def pe_scores(pe, b, s):
            if s >= 2:
                pe.wait_ge(sem("gated"), b * NB + s - 1)
            for n in range(2):
                last = pe.matmul(half(sc[s % 2], n), blk(kT, s), half(qT, n), start=True, stop=True)
            last.then_inc(sem("scores"), 1)

        def pe_retained(pe, b, t):
            if t == 0:
                pe.wait_ge(sem("v"), b + 1)
            pe.wait_ge(sem("gated"), b * NB + t + 1)
            r = D * (t % 2)
            for n in range(2):
                last = pe.matmul(half(ret, n)[r:r + D, :], v[:, t, :], gm[:, t % 2, n * TH:(n + 1) * TH],
                                 start=t < 2, stop=t >= NB - 2)
            last.then_inc(sem("ret"), 1)

        def pe_y(pe, b):
            pe.wait_ge(sem("retT"), b + 1)
            pe.matmul(vy[:], ones_row[:], bo_row[:], start=True, stop=False)
            for n in range(NB):
                last = pe.matmul(blk(vy, n, D), blk(retT, n), wo2[:], start=False, stop=n == NB - 1)
            last.then_inc(sem("y"), 1)

        def pe_h1T(pe, e, h):
            if h == 0:
                pe.wait_ge(sem("h1_twice"), e + 1)
                pe.wait_ge(sem("va"), e * 2 + 1)
            else:
                pe.wait_ge(sem("hT_low"), e * 2 + 1)
                pe.wait_ge(sem("hT_high"), e * 2 + 1)
            for n in range(NH):
                last = pe.transpose(blk(piece, n), h1[:, h * NH + n].rearrange("p a d -> p (a d)"), ident[:])
            last.then_inc(sem("h1T"), 1)

        def pe_convolution(pe, e):
            pe.wait_ge(sem("hT_low"), e * 2 + 2)
            pe.wait_ge(sem("hT_high"), e * 2 + 2)
            pe.matmul(piece[:], ones_row[:], cb_row[:], start=True, stop=False)
            for n in range(NB):
                for k in range(3):
                    last = pe.matmul(blk(piece, n, D), hT[:, n * P + 2 * k:n * P + 2 * k + P], cw[:, k, :],
                                     start=False, stop=n == NB - 1 and k == 2)
            last.then_inc(sem("z"), 1)

        def pe_nT(pe, e, h):
            if h == 0:
                pe.wait_ge(sem("ln"), e * 6 + 6)
            else:
                pe.wait_ge(sem("nT"), e * 2 + 1)
            alone(pe, sem)
            for n in range(NH):
                last = pe.transpose(blk(piece, n)[0:D, :], xc[:, h * NH + n, :], ident[:])
            last.then_inc(sem("nT_ps"), 1)

        def pe_qk(pe, e, h):
            if h == 0:
                pe.wait_ge(sem("nT"), e * 2 + 2)
            else:
                pe.wait_ge(sem("part0"), e * 2 + 1)
            pe.matmul(piece[:], wqk[:], half(nT, h), start=True, stop=True).then_inc(sem("qk2"), 1)

        def pe_va(pe, e, h):
            if h == 0:
                pe.wait_ge(sem("part0"), e * 2 + 2)
            else:
                pe.wait_ge(sem("va"), e * 2 + 1 + 1)
            for n in range(NH):
                last = pe.matmul(piece[:, n * P:n * P + H * VW], blk(nT, h * NH + n), wva[:], start=True, stop=True)
            last.then_inc(sem("va_ps"), 1)

        def pe_step(pe, b, e):
            if b is not None:
                pe_project(pe, b)
            for s in range(NB + 1):
                if b is not None:
                    if s < NB:
                        pe_scores(pe, b, s)
                    if s >= 1:
                        pe_retained(pe, b, s - 1)
                if e is not None:
                    if s < 2:
                        pe_h1T(pe, e, s)
                    elif s == 2:
                        pe_convolution(pe, e)
                    elif 4 <= s < 6:
                        pe_nT(pe, e, s - 4)
                    elif 6 <= s < 8:
                        pe_qk(pe, e, s - 6)
                    elif s == 8:
                        pe_va(pe, e, 0)
            if b is not None:
                pe_y(pe, b)
            if e is not None:
                pe_va(pe, e, 1)

        with nc.Block() as block:
            @block.sync
            def _(sp):
                for t, n in ((gammaT, "gammaT"), (wq, "wq"), (wk, "wk"), (wv, "wv"), (wo2, "wo2"), (bo_row, "bo_row"),
                             (cb_row, "cb_row"), (ones_row, "c_ones_row"), (beta, "beta"), (cw, "conv_w"),
                             (prelu, "prelu"), (eps, "c_eps12"), (ln_wb, "ln_wb"), (wqk, "wqk"), (wva, "wva"),
                             (qk_scale, "c_qk_scale")):
                    sp.dma_start(t[:], a[n]).then_inc(sem("weights"), 16)
                sp.sem_inc(sem("h1_stored"), 1)
                sp.sem_inc(sem("qk_stored"), 1)
                sp.sem_inc(sem("v_stored"), 1)
                load_x(sp, 0)
                load_x(sp, 1)
                store_h1(sp, 0)
                with sp.Fori(0, B - 2) as i:
                    load_x(sp, i + 2)
                    store_h1(sp, i + 1)
                    store_qkv(sp, i)
                store_h1(sp, B - 1)
                store_qkv(sp, B - 2)
                store_qkv(sp, B - 1)
                sp.wait_ge(sem("h1_stored"), 16 * B + 1)
                sp.wait_ge(sem("v_stored"), 16 * HP * B + 1)
                sp.wait_ge(sem("qk_stored"), 16 * 2 * NPART * B + 1)

            @block.gpsimd
            def _(pool):
                steps(pool, pool_step)

            @block.vector
            def _(dve):
                for t in (xT, nT, qT, kT):
                    dve.memset(t[D:KP, :], 0.0).then_inc(sem("pads"), 1)
                dve.memset(hT[:], 0.0).then_inc(sem("pads"), 1)
                dve.wait_ge(sem("pads"), 5)
                dve.memset(xT[D:D + 1, :], 1.0).then_inc(sem("pads"), 1)
                dve.memset(nT[D:D + 1, :], 1.0).then_inc(sem("pads"), 1)
                dve.wait_ge(sem("weights"), 16 * 16)
                dve.tensor_tensor(beta2[:, 0, :], beta[:], beta[:], ALU.mult).then_inc(sem("cw"), 1)
                dve.wait_ge(sem("cw"), 1)
                dve.tensor_scalar(beta2[:, 1, :], beta2[:, 0, :], 1.0, None, ALU.add).then_inc(sem("cw"), 1)
                dve.wait_ge(sem("cw"), 2)
                dve.tensor_scalar(beta2[:, 0, :], beta2[:, 0, :], -1.0, 1.0, ALU.mult, ALU.add).then_inc(sem("cw"), 1)
                dve.wait_ge(sem("cw"), 3)
                dve.tensor_tensor(cw[:], cw[:], beta2[:, 0:1, :].to_broadcast([P, 3, D]), ALU.mult).then_inc(sem("cw"), 1)
                dve.tensor_tensor(beta[0:D, :], ident[0:D, 0:D], beta2[0:D, 1, :], ALU.mult).then_inc(sem("cw"), 1)
                dve.wait_ge(sem("cw"), 5)
                dve.tensor_tensor(cw[0:D, 2, :], cw[0:D, 2, :], beta[0:D, :], ALU.add).then_inc(sem("cw"), 1)
                dve.tensor_tensor(cb_row[:].rearrange("p (n d) -> p n d", d=D), cb_row[:].rearrange("p (n d) -> p n d", d=D),
                                  beta2[0:KP, 0:1, :].to_broadcast([KP, NB, D]), ALU.mult).then_inc(sem("cw"), 1)
                dve.wait_ge(sem("pads"), 7)
                steps(dve, dve_step)

            @block.scalar
            def _(act):
                act.sem_inc(sem("va"), 1)
                act.wait_ge(sem("weights"), 16 * 16)
                act.wait_ge(sem("pads"), 7)
                steps(act, act_step)

            @block.tensor
            def _(pe):
                pe.sem_inc(sem("v_proj"), 1)
                pe.wait_ge(sem("weights"), 16 * 16)
                pe.wait_ge(sem("pads"), 7)
                pe.wait_ge(sem("cw"), 7)
                steps(pe, pe_step)


def attention_phase(nc, a, st, hold):
    ident, identb, maskb, pos = hold["ident"], hold["identb"], hold["maskb"], hold["pos"]
    with ExitStack() as c:
        sb = lambda n, s, d=F32: c.enter_context(nc.sbuf_tensor(n, s, d))
        names = {}

        def sem(n):
            if n not in names:
                names[n] = c.enter_context(nc.semaphore("b_" + n))
            return names[n]

        qs = [[sb(f"qs{p}{g}", [KP, T], BF16) for g in range(G)] for p in range(2)]
        ks = [[sb(f"ks{p}{g}", [KP, T], BF16) for g in range(G)] for p in range(2)]
        xe = [sb(f"xe{p}", [P, G * HEADW]) for p in range(2)]
        vals = [sb(f"vals{p}", [P, NB, G * VW]) for p in range(2)]
        limit = [sb(f"limit{p}", [P, G]) for p in range(2)]
        rate = [sb(f"rate{p}", [P, G]) for p in range(2)]
        negmax, rtot, max2 = sb("negmax", [P, 2, NU]), sb("rtot", [P, 2, NU]), sb("max2", [P, 2, NU])
        behind = sb("behind", [P, NBEHIND, T // 2 + 1])
        pt = [sb(f"pt{i}", [P, 512]) for i in range(NPT)]
        ot = [sb(f"ot{i}", [P, 512]) for i in range(2)]
        o = sb("o", [P, G, NB, VW])
        s1 = [c.enter_context(nc.psum_tensor(f"s1_{i}", [P, max(WIDTH[i::2])], F32)) for i in range(2)]
        s2 = c.enter_context(nc.psum_tensor("s2", [P, T], F32))
        tp = [c.enter_context(nc.psum_tensor(f"tp{i}", [P, 512], F32)) for i in range(2)]
        op = c.enter_context(nc.psum_tensor("op", [P, 512], F32))

        def group(i, c):
            if isinstance(i, int) and not 0 <= 2 * i + c < NSTEP:
                return None
            return Group(i * 2 + c, c % 2, i + c // 2)

        def at(i, c, s, delay):
            d, u = divmod(s - delay, NU)
            return group(i, c + d), u

        def due(i, c, s, slots):
            units = [(group(i, c - t // NU), u) for u, t in enumerate(slots) if t % NU == s]
            return sorted(((m, u) for m, u in units if m), key=lambda x: slots[x[1]], reverse=True)

        def span(m, u, k0=0, k1=None):
            return xe[m.p][:, START[u] + k0:START[u] + (WIDTH[u] if k1 is None else k1)]

        def plane(m, u, odd):
            return xe[m.p][:, START[u] + odd:START[u] + WIDTH[u]:2]

        def tail(u, shift):
            h = WIDTH[u] // 2
            return behind[:, u % NBEHIND, T // 2 - h + shift:T // 2 + shift]

        def scores(pe, dst, m, u):
            g, qb = UNITS[u]
            w = WIDTH[u]
            q = qs[m.p][g][:, qb * P:(qb + 1) * P]
            for lo in range(0, w, 512):
                hi = min(lo + 512, w)
                pe.matmul(dst[:, lo:hi], q, ks[m.p][g][:, lo:hi], start=True, stop=hi < w)
            return pe.matmul(dst[:, w - P:w], identb[:], maskb[:], start=False, stop=True)

        def pe_front(pe, m, u):
            if u % NB == 0:
                pe.wait_ge(sem(f"qk_loaded{UNITS[u][0]}{m.p}"), m.turn * 32 * NPART + 32 * NPART)
            if not first(m) or u >= 2:
                pe.wait_ge(sem("exp1"), m.n * NU + u - 1)
            scores(pe, s1[u % 2], m, u).then_inc(sem("scores1"), 1)

        def pe_back(pe, m, u):
            pe.wait_ge(sem("weighted"), m.n * NU + u + 1)
            scores(pe, s2, m, u).then_inc(sem("scores2"), 1)

        def pe_values(pe, m, k):
            u, j0, n = TILES[k]
            g, qb = UNITS[u]
            pe.wait_ge(sem("exp2"), m.n * NT + k + 1)
            if k == 0:
                pe.wait_ge(sem(f"v_loaded{m.p}"), m.turn * 16 + 16)
            if j0 == 0 and u % 4 == 0:
                pe.wait_ge(sem("ot"), m.n * NQ + u // 4 + 1)
            for i in range(n):
                j = j0 + i
                last = pe.matmul(op[32 * i:32 * i + VW, (u % 4) * P:(u % 4 + 1) * P],
                                 vals[m.p][:, j, g * VW:(g + 1) * VW], pt[k % NPT][:, i * P:(i + 1) * P],
                                 start=j0 == 0, stop=j + 4 > qb)
            last.then_inc(sem("products"), 1)

        def pe_transposes(pe, m, before, u):
            acts = up_to(NU - 1, act_shifts)
            if act_shifts(u):
                pe.wait_ge(sem("act_shifted"), m.n * acts + up_to(u, act_shifts))
            else:
                pe.wait_ge(sem("pool_shifted"), m.n * (NU - acts) + u + 1 - up_to(u, act_shifts))
            if u % 4 == 2 and (u > 2 or not first(m)):
                pe.wait_ge(sem("o"), m.n * NU + 4 * (u // 4) + 1)
            for k in tiles_of(u):
                _, j0, n = TILES[k]
                if not first(m) or k > 1:
                    pe.wait_ge(sem("exp2"), m.n * NT + k - 1)
                for i in range(n):
                    last = pe.transpose(tp[k % 2][:, i * P:(i + 1) * P], span(m, u, (j0 + i) * P, (j0 + i + 1) * P), ident[:])
                last.then_inc(sem("transposed"), 1)
                if k >= TILES_BEHIND:
                    pe_values(pe, m, k - TILES_BEHIND)
                elif before is not None:
                    pe_values(pe, before, k - TILES_BEHIND + NT)

        def pe_rows(pe, m, q, read):
            pe.wait_ge(sem("ot"), m.n * NQ + q + 1 + 1)
            pe.wait_ge(sem("exp2"), m.n * NT + read)
            for i in range(4):
                last = pe.transpose(tp[rows_bank(q)][:, i * P:(i + 1) * P], ot[q % 2][:, i * P:(i + 1) * P], ident[:])
            last.then_inc(sem("rows"), 1)

        def pe_step(pe, i, c):
            for s in range(NU):
                back, v = at(i, c, s, SCORES2)
                if back:
                    pe_back(pe, back, v)
                m, u = at(i, c, s, SUM)
                before, _ = at(i, c, s, SUM + NU)
                if m:
                    pe_transposes(pe, m, before, u)
                elif before and last(before) and u == 0:
                    for k in range(NT - TILES_BEHIND, NT):
                        pe_values(pe, before, k)
                front, v = at(i, c, s, 0)
                if front:
                    pe_front(pe, front, v)
                if m and u % 4 == 1 and u > 1:
                    pe_rows(pe, m, u // 4 - 1, tiles_of(u)[-1])
                elif before and u == 1:
                    pe_rows(pe, before, NQ - 1, NT + tiles_of(u)[-1] if m else NT)

        def act_copy_products(act, m, q):
            act.wait_ge(sem("products"), m.n * NT + tiles_of(4 * q + 3)[-1] + 1)
            act.copy(ot[q % 2][:], op[:]).then_inc(sem("ot"), 1)

        def act_step(act, i, c):
            for s in range(NU):
                m, u = at(i, c, s, EXP2)
                if m:
                    for k in tiles_of(u):
                        n = TILES[k][2]
                        act.wait_ge(sem("transposed"), m.n * NT + k + 1)
                        if not first(m) or k >= NPT:
                            act.wait_ge(sem("products"), m.n * NT + k - NPT + 1)
                        act.activation(pt[k % NPT][:, 0:n * P], tp[k % 2][:, 0:n * P], ACT.Exp, scale=-1.0).then_inc(sem("exp2"), 1)
                m, u = at(i, c, s, SUM)
                before, _ = at(i, c, s, SUM + NU)
                if u == 1 and before:
                    act_copy_products(act, before, NQ - 1)
                elif u % 4 == 1 and u > 1 and m:
                    act_copy_products(act, m, u // 4 - 1)
                m, u = at(i, c, s, EXP)
                if m:
                    act.wait_ge(sem("negmax"), m.n * NU + u + 1)
                    act.activation(span(m, u), s1[u % 2][:, 0:WIDTH[u]], ACT.Exp,
                                   bias=negmax[:, m.p, u:u + 1]).then_inc(sem("exp1"), 1)
                if s == SQRT_SLOT and group(i, c - 1):
                    m = group(i, c - 1)
                    for g in range(G):
                        act.wait_ge(sem("clipped"), m.n * NU + NB * (g + 1))
                        act.activation(head(xe[m.p], g), head(xe[m.p], g), ACT.Sqrt).then_inc(sem("dist"), 1)
                m, u = at(i, c, s, EFFECT)
                if m and u % 2 == 0:
                    g = u // NB
                    act.wait_ge(sem("dist"), m.n * G + g + 1)
                    if u == 0:
                        act.wait_ge(sem(f"rate_loaded{m.p}"), m.turn * 16 + 16)
                    two = xe[m.p][:, START[u]:START[u + 1] + WIDTH[u + 1]]
                    act.activation(two, two, ACT.Exp, scale=rate[m.p][:, g:g + 1]).then_inc(sem("effect"), 1)
                m, u = at(i, c, s, WEIGH)
                if m and act_shifts(u):
                    act.wait_ge(sem("weighted"), m.n * NU + u + 1 + 1)
                    act.activation(span(m, u), span(m, u), ACT.Identity, scale=-1.0, bias=max2[:, m.p, u:u + 1]).then_inc(sem("act_shifted"), 1)

        def dve_rows(dve, m, q):
            dve.wait_ge(sem("rows"), m.n * NQ + q + 1)
            if q == 0:
                dve.wait_ge(sem("o_stored"), m.n * 16 + 1)
            for i in range(4):
                g, qb = UNITS[4 * q + i]
                dve.tensor_reduce(o[:, g, qb, :], tp[rows_bank(q)][:, i * P:(i + 1) * P].rearrange("p (j d) -> p d j", d=32)[:, 0:VW, 0:min(4, qb + 1)],
                                  AX.X, ALU.add).then_inc(sem("o"), 1)

        def dve_step(dve, i, c):
            for s in range(NU):
                m, u = at(i, c, s, SUM)
                before, _ = at(i, c, s, SUM + NU)
                if u == 2 and before:
                    dve_rows(dve, before, NQ - 1)
                elif u % 4 == 2 and u > 2 and m:
                    dve_rows(dve, m, u // 4 - 1)
                m, u = at(i, c, s, WEIGH)
                if m:
                    dve.wait_ge(sem("effect"), m.n * (NU // 2) + u // 2 + 1)
                    dve.wait_ge(sem("scores2"), m.n * NU + u + 1)
                    alone(dve, sem)
                    dve.tensor_tensor_reduce(out=span(m, u), in0=span(m, u), in1=s2[:, 0:WIDTH[u]], scale=1.0, scalar=-3.4e38,
                                             op0=ALU.mult, op1=ALU.max, accum_out=max2[:, m.p, u:u + 1]).then_inc(sem("weighted"), 1)
                m, u = at(i, c, s, MAX)
                if m:
                    dve.wait_ge(sem("scores1"), m.n * NU + u + 1)
                    dve.tensor_reduce(negmax[:, m.p, u:u + 1], s1[u % 2][:, 0:WIDTH[u]], AX.X, ALU.max,
                                      negate=True).then_inc(sem("negmax"), 1)
                scanned = due(i, c, s, SCAN)
                for m, u in scanned:
                    dve.wait_ge(sem("exp1"), m.n * NU + u + 1)
                    dve.tensor_tensor_scan(tail(u, 0)[:, ::-1], plane(m, u, 1)[:, ::-1], plane(m, u, 0)[:, ::-1],
                                           0.0, ALU.add, ALU.add).then_inc(sem("scan"), 1)
                for m, u in due(i, c, s, CLIP):
                    if not pool_takes_odd(u):
                        dve.wait_ge(sem("added"), m.n * NU + u + 1)
                        dve.tensor_tensor(plane(m, u, 1), tail(u, 1), pos[:, T - WIDTH[u] + 1:T:2], ALU.mult).then_inc(sem("far_odd"), 1)
                for m, u in scanned:
                    dve.wait_ge(sem("scan"), m.n * NU + u + 1)
                    dve.reciprocal(rtot[:, m.p, u:u + 1], tail(u, 0)[:, 0:1]).then_inc(sem("rtot"), 1)
                for m, u in due(i, c, s, CLIP):
                    if u == 0:
                        dve.wait_ge(sem(f"limit_loaded{m.p}"), m.turn * 16 + 16)
                    dve.wait_ge(sem("rtot"), m.n * NU + u + 1)
                    if not pool_takes_odd(u):
                        dve.wait_ge(sem("far_odd"), m.n * (NU - up_to(NU - 1, pool_takes_odd)) + u + 1 - up_to(u, pool_takes_odd))
                    dve.wait_ge(sem("far"), m.n * NU + u + 1)
                    dve.tensor_scalar(span(m, u), span(m, u), rtot[:, m.p, u:u + 1], limit[m.p][:, UNITS[u][0]:UNITS[u][0] + 1],
                                      ALU.mult, ALU.min).then_inc(sem("clipped"), 1)

        def pool_step(pool, i, c):
            for s in range(NU):
                m, u = at(i, c, s, WEIGH)
                if m and not act_shifts(u):
                    pool.wait_ge(sem("weighted"), m.n * NU + u + 1 + 1)
                    alone(pool, sem)
                    pool.tensor_scalar(span(m, u), span(m, u), -1.0, max2[:, m.p, u:u + 1], ALU.mult, ALU.add).then_inc(sem("pool_shifted"), 1)
                for m, u in due(i, c, s, SCAN):
                    pool.wait_ge(sem("scan"), m.n * NU + u + 1)
                    pool.tensor_tensor(plane(m, u, 0), tail(u, 1), plane(m, u, 1), ALU.add).then_inc(sem("added"), 1)
                    pool.wait_ge(sem("added"), m.n * NU + u + 1)
                    if pool_takes_odd(u):
                        pool.tensor_tensor(plane(m, u, 1), tail(u, 1), pos[:, T - WIDTH[u] + 1:T:2], ALU.mult)
                    pool.tensor_tensor(plane(m, u, 0), plane(m, u, 0), pos[:, T - WIDTH[u]:T:2], ALU.mult).then_inc(sem("far"), 1)

        def load_qk(sp, m, g):
            heads = st["qk"][DS((m.n * G + g) * DK, DK)].rearrange("d w r t -> w r d t")
            for r in range(NPART):
                to = slice(r * NPART * DK, (r + 1) * NPART * DK)
                sp.dma_start(qs[m.p][g][to, :], heads[0, r].unsqueeze(0).to_broadcast([NPART, DK, T])).then_inc(sem(f"qk_loaded{g}{m.p}"), 16)
                sp.dma_start(ks[m.p][g][to, :], heads[1]).then_inc(sem(f"qk_loaded{g}{m.p}"), 16)

        def load_limit(sp, m):
            sp.dma_start(limit[m.p][:], st["par"][DS(m.n, 1), 1].rearrange("a p g -> (a p) g")).then_inc(sem(f"limit_loaded{m.p}"), 16)

        def load_rate(sp, m):
            sp.dma_start(rate[m.p][:], st["par"][DS(m.n, 1), 0].rearrange("a p g -> (a p) g")).then_inc(sem(f"rate_loaded{m.p}"), 16)

        def load_values(sp, m):
            sp.dma_start(vals[m.p][:], st["v"][DS(m.n, 1)].rearrange("a p n w -> (a p) n w")).then_inc(sem(f"v_loaded{m.p}"), 16)

        def sp_step(sp, i, c):
            old, before, m, following = (group(i, c + d) for d in (-2, -1, 0, 1))
            if following and before:
                sp.wait_ge(sem("clipped"), before.n * NU + NU)
                alone(sp, sem)
                load_limit(sp, following)
            if old and m:
                sp.wait_ge(sem("scores2"), old.n * NU + NU)
                alone(sp, sem)
                load_qk(sp, m, 1)
                sp.wait_ge(sem("effect"), old.n * (NU // 2) + NU // 2)
                alone(sp, sem)
                load_rate(sp, m)
                sp.wait_ge(sem("products"), old.n * NT + NT)
                alone(sp, sem)
                load_values(sp, m)
            if old:
                sp.wait_ge(sem("o"), old.n * NU + NU + 1)
                alone(sp, sem)
                sp.dma_start(st["o"][DS(old.n, 1)].rearrange("a p w -> (a p) w"), o[:].rearrange("p g n d -> p (g n d)")).then_inc(sem("o_stored"), 16)
            if following and before:
                sp.wait_ge(sem("scores2"), before.n * NU + NB)
                alone(sp, sem)
                load_qk(sp, following, 0)

        def steps(eng, step):
            step(eng, 0, 0)
            step(eng, 0, 1)
            with eng.Fori(0, (NSTEP - 4) // 2) as i:
                step(eng, i, 2)
                step(eng, i, 3)
            for m in range(NSTEP - 2, NSTEP + 2):
                step(eng, m // 2, m % 2)

        with nc.Block() as block:
            @block.sync
            def _(sp):
                sp.sem_inc(sem("o_stored"), 1)
                sp.wait_ge(sem("pads"), 4 * G)
                for n in range(2):
                    m = group(0, n)
                    for g in range(G):
                        load_qk(sp, m, g)
                    load_limit(sp, m)
                    load_rate(sp, m)
                    load_values(sp, m)
                steps(sp, sp_step)
                sp.wait_ge(sem("o_stored"), 16 * NSTEP + 1)

            @block.gpsimd
            def _(pool):
                steps(pool, pool_step)

            @block.vector
            def _(dve):
                for p in range(2):
                    for g in range(G):
                        dve.memset(qs[p][g][D:KP, :], 0.0).then_inc(sem("pads"), 1)
                        dve.memset(ks[p][g][D:KP, :], 0.0).then_inc(sem("pads"), 1)
                dve.memset(op[:], 0.0).then_inc(sem("cleared"), 1)
                dve.memset(behind[:, :, T // 2:T // 2 + 1], 0.0).then_inc(sem("cleared"), 1)
                dve.sem_inc(sem("weighted"), 1)
                dve.sem_inc(sem("o"), 1)
                steps(dve, dve_step)

            @block.scalar
            def _(act):
                act.sem_inc(sem("ot"), 1)
                steps(act, act_step)

            @block.tensor
            def _(pe):
                pe.wait_ge(sem("cleared"), 2)
                steps(pe, pe_step)


def channel_phase(nc, a, st, hold, out):
    ident = hold["ident"]
    with ExitStack() as c:
        sb = lambda n, s, d=F32: c.enter_context(nc.sbuf_tensor(n, s, d))
        names = {}

        def sem(n):
            if n not in names:
                names[n] = c.enter_context(nc.semaphore("c_" + n))
            return names[n]

        NC = E * HID // P
        ow, rw = sb("ow", [KP, D]), sb("rw", [KP, E])
        w1 = sb("w1", [KP, E * HID])
        w2 = sb("w2", [P, NC, D])
        b2 = sb("b2", [KP, D])
        expandf = sb("expandf", [KP, E * HID])
        expand = sb("expand", [KP, E * HID], BF16)
        prio = sb("prio", [P, E])
        rowmask = sb("rowmask", [P, 1])
        eps = sb("eps5", [P, 1])
        os_ = sb("os", [P, H, NB, VW])
        rden = sb("rden", [P, H, NB])
        att = sb("att", [P, NB, H, DK])
        aT = sb("aT", [KP, T])
        h1 = sb("h1c", [P, NB, D])
        res = sb("res", [P, NB, D])
        xc, sq = sb("xc2", [P, NB, D]), sb("sq2", [P, NB, D])
        stat = sb("stat2", [P, 4, NB])
        h2, h2_kept = sb("h2", [P, NB, D]), sb("h2_kept", [P, NB, D])
        h2T = sb("h2T", [KP, T])
        best = sb("best", [P, 2, NB])
        hot = sb("hot", [P, NB, E])
        rank = sb("rank", [P, NB, E])
        hotT = sb("hotT", [KP, T])
        coldT = sb("coldT", [KP, T], BF16)
        hid = sb("hid", [P, 2, T])
        fT = sb("fT", [D, T])
        y = sb("y", [P, NB, D])
        hidden = [c.enter_context(nc.psum_tensor(f"c_hidden{i}", [P, T], F32)) for i in range(2)]
        mixed = c.enter_context(nc.psum_tensor("c_mixed", [D, T], F32))
        expert_rows = c.enter_context(nc.psum_tensor("c_expert_rows", [P, NB * D], F32))
        piece = c.enter_context(nc.psum_tensor("c_piece", [P, T // 2], F32))
        TH, NH = T // 2, NB // 2
        half = lambda t, i: t[:, i * TH:(i + 1) * TH]
        blk = lambda t, i, w=P: t[:, i * w:(i + 1) * w]
        rows = lambda t: t[:].rearrange("p (n d) -> p n d", d=D)

        def steps(eng, step):
            step(eng, 0, None)
            with eng.Fori(0, B - 1) as i:
                step(eng, i + 1, i)
            step(eng, None, B - 1)

        def load(sp, b):
            if not isinstance(b, int) or b > 0:
                sp.wait_ge(sem("att"), b)
                alone(sp, sem)
            sp.dma_start(os_[:].rearrange("p (s g) n d -> p s (g n d)", g=G),
                         st["o"][DS(b * HP, HP)].rearrange("s p w -> p s w")).then_inc(sem("o_loaded"), 16)
            if not isinstance(b, int) or b > 0:
                sp.wait_ge(sem("res"), b)
                alone(sp, sem)
            sp.dma_start(h1[:], st["h1"][DS(b, 1)].rearrange("a p n d -> (a p) n d")).then_inc(sem("h1_loaded"), 16)

        def store(sp, e):
            sp.wait_ge(sem("y"), e + 1)
            alone(sp, sem)
            sp.dma_start(out[DS(e, 1)].rearrange("a (n p) d -> (a p) n d", p=P), y[:]).then_inc(sem("stored"), 16)

        def centre(dve, x, n, which):
            ln = sem("ln" + which)
            dve.tensor_reduce(stat[:, 0, :], x, AX.X, ALU.add).then_inc(ln, 1)
            dve.wait_ge(ln, n * 5 + 1)
            dve.tensor_scalar(stat[:, 1, :], stat[:, 0, :], -1.0 / D, None, ALU.mult).then_inc(ln, 1)
            dve.wait_ge(ln, n * 5 + 2)
            dve.tensor_tensor(xc[:], x, stat[:, 1, :].unsqueeze(2).to_broadcast([P, NB, D]), ALU.add).then_inc(ln, 1)
            dve.wait_ge(ln, n * 5 + 3)
            dve.tensor_tensor(sq[:], xc[:], xc[:], ALU.mult).then_inc(ln, 1)
            dve.wait_ge(ln, n * 5 + 4)
            dve.tensor_reduce(stat[:, 2, :], sq[:], AX.X, ALU.add).then_inc(sem("var" + which), 1)

        def scale(dve, to, n, which, done):
            ln = sem("ln" + which)
            dve.wait_ge(sem("std" + which), n + 1)
            dve.reciprocal(stat[:, 1, :], stat[:, 3, :]).then_inc(ln, 1)
            dve.wait_ge(ln, n * 5 + 5)
            dve.tensor_tensor(to, xc[:], stat[:, 1, :].unsqueeze(2).to_broadcast([P, NB, D]), ALU.mult).then_inc(done, 1)

        def dve_step(dve, b, e):
            if b is not None:
                dve.wait_ge(sem("o_loaded"), b * 16 + 16)
                dve.reciprocal(rden[:], os_[:, :, :, DK]).then_inc(sem("rden"), 1)
                dve.wait_ge(sem("rden"), b * 2 + 1)
                dve.tensor_scalar(rden[:, :, 0], rden[:, :, 0], rowmask[:, 0:1], None, ALU.mult).then_inc(sem("rden"), 1)
                dve.wait_ge(sem("rden"), b * 2 + 2)
                dve.tensor_tensor(att[:].rearrange("p n h d -> p h n d"), os_[:, :, :, 0:DK],
                                  rden[:].unsqueeze(3).to_broadcast([P, H, NB, DK]), ALU.mult).then_inc(sem("att"), 1)
                dve.wait_ge(sem("attended"), b + 1)
                dve.wait_ge(sem("h1_loaded"), b * 16 + 16)
                dve.tensor_tensor(res[:], rows(piece), h1[:], ALU.add).then_inc(sem("res"), 1)
                dve.wait_ge(sem("res"), b + 1)
                centre(dve, res[:], b, "1")
                if e is not None:
                    dve.wait_ge(sem("kept"), e + 1)
                scale(dve, h2[:], b, "1", sem("h2"))
                dve.wait_ge(sem("logits"), b + 1)
                logits = piece[:, 0:NB * E].rearrange("p (n e) -> p n e", e=E)
                dve.tensor_reduce(best[:, 0, :], logits, AX.X, ALU.max).then_inc(sem("hot"), 1)
                dve.wait_ge(sem("hot"), b * 5 + 1)
                dve.tensor_tensor(rank[:], logits, best[:, 0, :].unsqueeze(2).to_broadcast([P, NB, E]), ALU.is_ge).then_inc(sem("hot"), 1)
                dve.wait_ge(sem("hot"), b * 5 + 2)
                dve.tensor_tensor(rank[:], rank[:], prio[:].unsqueeze(1).to_broadcast([P, NB, E]), ALU.mult).then_inc(sem("hot"), 1)
                dve.wait_ge(sem("hot"), b * 5 + 3)
                dve.tensor_reduce(best[:, 1, :], rank[:], AX.X, ALU.max).then_inc(sem("hot"), 1)
                dve.wait_ge(sem("hot"), b * 5 + 4)
                dve.tensor_tensor(hot[:], rank[:], best[:, 1, :].unsqueeze(2).to_broadcast([P, NB, E]), ALU.is_equal).then_inc(sem("hot"), 1)
            if e is not None:
                dve.wait_ge(sem("experts"), e + 1)
                dve.wait_ge(sem("kept"), e + 1)
                dve.tensor_tensor(res[:], rows(expert_rows), h2_kept[:], ALU.add).then_inc(sem("res2"), 1)
                dve.wait_ge(sem("res2"), e + 1 + 1)
                centre(dve, res[:], e, "2")
            if b is not None:
                for h in range(2):
                    dve.wait_ge(sem("hotT_ps"), b * 2 + h + 1)
                    dve.tensor_copy(half(hotT, h)[0:E, :], piece[0:E, :]).then_inc(sem("hotT"), 1)
                dve.wait_ge(sem("hotT"), b * 2 + 2)
                dve.tensor_scalar(coldT[0:E, :], hotT[0:E, :], -1.0, None, ALU.add).then_inc(sem("coldT"), 1)
            if e is not None:
                dve.wait_ge(sem("stored"), e * 16 + 1)
                scale(dve, y[:], e, "2", sem("y"))

        def pool_step(pool, b, e):
            if b is not None:
                pool.wait_ge(sem("h2"), b + 1)
                if e is not None:
                    pool.wait_ge(sem("res2"), e + 1 + 1)
                alone(pool, sem)
                pool.tensor_copy(h2_kept[:], h2[:]).then_inc(sem("kept"), 1)

        def act_aT(act, b, h):
            act.wait_ge(sem("aT_ps"), b * 2 + h + 1)
            act.copy(half(aT, h)[0:D, :], piece[0:D, :]).then_inc(sem("aT"), 1)

        def act_std(act, n, which):
            act.wait_ge(sem("var" + which), n + 1)
            act.activation(stat[:, 3, :], stat[:, 2, :], ACT.Sqrt, scale=1.0 / D, bias=eps[:, 0:1]).then_inc(sem("std" + which), 1)

        def act_relu(act, e, i):
            act.wait_ge(sem("hidden"), e * NC + i + 1)
            if i >= 2:
                act.wait_ge(sem("mixed"), e * NC + i - 1)
            act.activation(hid[:, i % 2, :], hidden[i % 2][:], ACT.Relu).then_inc(sem("relu"), 1)

        def act_step(act, b, e):
            for h in range(2):
                if b is not None:
                    act_aT(act, b, h)
                if e is not None:
                    act_relu(act, e, h)
            if e is not None:
                act_relu(act, e, 2)
            if b is not None:
                act_std(act, b, "1")
            if e is not None:
                act_relu(act, e, 3)
            if b is not None:
                for h in range(2):
                    act.wait_ge(sem("h2T_ps"), b * 2 + h + 1)
                    act.copy(half(h2T, h)[0:D, :], piece[0:D, :]).then_inc(sem("h2T"), 1)
            if e is not None:
                act.wait_ge(sem("mixed"), e * NC + NC)
                act.activation(fT[:], mixed[:], ACT.Relu).then_inc(sem("fT"), 1)
                act_std(act, e, "2")

        def pe_aT(pe, b, h):
            if h == 1:
                pe.wait_ge(sem("aT"), b * 2 + 1)
            else:
                if not isinstance(b, int):
                    pe.wait_ge(sem("hotT"), b * 2)
                pe.wait_ge(sem("att"), b + 1)
            alone(pe, sem)
            for n in range(NH):
                last = pe.transpose(blk(piece, n)[0:D, :], att[:, h * NH + n].rearrange("p h d -> p (h d)"), ident[:])
            last.then_inc(sem("aT_ps"), 1)

        def pe_attended(pe, b):
            pe.wait_ge(sem("aT"), b * 2 + 2)
            for n in range(NB):
                last = pe.matmul(blk(piece, n, D), blk(aT, n), ow[:], start=True, stop=True)
            last.then_inc(sem("attended"), 1)

        def pe_h2T(pe, b, h):
            if h == 1:
                pe.wait_ge(sem("h2T"), b * 2 + 1)
            else:
                pe.wait_ge(sem("h2"), b + 1)
            alone(pe, sem)
            for n in range(NH):
                last = pe.transpose(blk(piece, n)[0:D, :], h2[:, h * NH + n, :], ident[:])
            last.then_inc(sem("h2T_ps"), 1)

        def pe_logits(pe, b):
            pe.wait_ge(sem("h2T"), b * 2 + 2)
            for n in range(NB):
                last = pe.matmul(blk(piece, n, E), blk(h2T, n), rw[:], start=True, stop=True)
            last.then_inc(sem("logits"), 1)

        def pe_hotT(pe, b, h):
            if h == 1:
                pe.wait_ge(sem("hotT"), b * 2 + 1)
            else:
                pe.wait_ge(sem("hot"), b * 5 + 5)
            alone(pe, sem)
            for n in range(NH):
                last = pe.transpose(blk(piece, n)[0:E, :], hot[:, h * NH + n, :], ident[:])
            last.then_inc(sem("hotT_ps"), 1)

        def pe_hidden(pe, e, i):
            if i == 0:
                pe.wait_ge(sem("coldT"), e + 1)
            if i >= 2:
                pe.wait_ge(sem("relu"), e * NC + i - 1)
            for n in range(2):
                dst = half(hidden[i % 2], n)
                pe.matmul(dst, blk(w1, i), half(h2T, n), start=True, stop=False)
                last = pe.matmul(dst, blk(expand, i), half(coldT, n), start=False, stop=True)
            last.then_inc(sem("hidden"), 1)

        def pe_mixed(pe, e, i):
            if i == 0:
                pe.wait_ge(sem("hotT"), e * 2 + 2)
                pe.wait_ge(sem("fT"), e + 1)
                for n in range(2):
                    pe.matmul(half(mixed, n), b2[:], half(hotT, n), start=True, stop=False)
            pe.wait_ge(sem("relu"), e * NC + i + 1)
            for n in range(2):
                last = pe.matmul(half(mixed, n), w2[:, i, :], hid[:, i % 2, n * TH:(n + 1) * TH],
                                 start=False, stop=i == NC - 1)
            last.then_inc(sem("mixed"), 1)

        def pe_experts(pe, e):
            pe.wait_ge(sem("fT"), e + 1 + 1)
            pe.wait_ge(sem("res2"), e + 1)
            alone(pe, sem)
            for n in range(NB):
                last = pe.transpose(blk(expert_rows, n, D), blk(fT, n), ident[0:D, 0:D])
            last.then_inc(sem("experts"), 1)

        def pe_step(pe, b, e):
            for h in range(2):
                if b is not None:
                    pe_aT(pe, b, h)
                if e is not None:
                    pe_hidden(pe, e, h)
            if b is not None:
                pe_attended(pe, b)
            if e is not None:
                pe_mixed(pe, e, 0)
                pe_hidden(pe, e, 2)
                pe_mixed(pe, e, 1)
                pe_hidden(pe, e, 3)
            for h in range(2):
                if b is not None:
                    pe_h2T(pe, b, h)
                if e is not None:
                    pe_mixed(pe, e, 2 + h)
            if b is not None:
                pe_logits(pe, b)
            if e is not None:
                pe_experts(pe, e)
            if b is not None:
                for h in range(2):
                    pe_hotT(pe, b, h)

        with nc.Block() as block:
            @block.sync
            def _(sp):
                for t, n in ((ow, "ow"), (rw, "rw"), (w1, "w1"), (w2, "w2"), (b2, "b2"), (expandf, "c_expand"),
                             (prio, "c_prio"), (rowmask, "c_rowmask"), (eps, "c_eps5")):
                    sp.dma_start(t[:], a[n]).then_inc(sem("weights"), 16)
                sp.sem_inc(sem("stored"), 1)
                load(sp, 0)
                load(sp, 1)
                with sp.Fori(0, B - 2) as i:
                    load(sp, i + 2)
                    store(sp, i)
                store(sp, B - 2)
                store(sp, B - 1)
                sp.wait_ge(sem("stored"), 16 * B + 1)

            @block.gpsimd
            def _(pool):
                steps(pool, pool_step)

            @block.vector
            def _(dve):
                for t in (aT, h2T):
                    dve.memset(t[D:KP, :], 0.0).then_inc(sem("pads"), 1)
                dve.memset(hotT[:], 0.0).then_inc(sem("pads"), 1)
                dve.memset(coldT[:], 0.0).then_inc(sem("pads"), 1)
                dve.wait_ge(sem("pads"), 4)
                dve.memset(aT[D:D + 1, :], 1.0).then_inc(sem("pads"), 1)
                dve.memset(h2T[D:D + 1, :], 1.0).then_inc(sem("pads"), 1)
                dve.wait_ge(sem("weights"), 16 * 9)
                dve.tensor_copy(expand[:], expandf[:]).then_inc(sem("expand"), 1)
                dve.sem_inc(sem("res2"), 1)
                dve.wait_ge(sem("pads"), 6)
                steps(dve, dve_step)

            @block.scalar
            def _(act):
                act.sem_inc(sem("fT"), 1)
                act.wait_ge(sem("weights"), 16 * 9)
                act.wait_ge(sem("pads"), 6)
                steps(act, act_step)

            @block.tensor
            def _(pe):
                pe.wait_ge(sem("weights"), 16 * 9)
                pe.wait_ge(sem("pads"), 6)
                pe.wait_ge(sem("expand"), 1)
                steps(pe, pe_step)


def program(nc, a, out):
    st = {
        "par": nc.dram_tensor("step_par", [NSTEP, 2, P, G], F32).ap(),
        "h1": nc.dram_tensor("tok_rows", [B, P, NB, D], F32).ap(),
        "v": nc.dram_tensor("value_rows", [NSTEP, P, NB, G * VW], F32).ap(),
        "qk": nc.dram_tensor("qk_parts", [B * H * DK, 2, NPART, T], BF16).ap(),
        "o": nc.dram_tensor("attended_rows", [NSTEP, P, G * NB * VW], F32).ap(),
    }
    with ExitStack() as c:
        hold = {
            "ident": c.enter_context(nc.sbuf_tensor("ident", [P, P], F32)),
            "identb": c.enter_context(nc.sbuf_tensor("identb", [P, P], BF16)),
            "maskb": c.enter_context(nc.sbuf_tensor("maskb", [P, P], BF16)),
            "pos": c.enter_context(nc.sbuf_tensor("pos", [P, T], F32)),
            "gam": c.enter_context(nc.sbuf_tensor("gam", [P, H], F32)),
        }
        setup_phase(nc, a, st, hold)
        token_phase(nc, a, st, hold)
        attention_phase(nc, a, st, hold)
        channel_phase(nc, a, st, hold, out)


def kernel(**inputs):
    import numpy as np
    import concourse.bacc as bacc
    from concourse.bass_utils import run_bass_kernel_spmd

    f = np.float32
    i = {n: np.asarray(x) for n, x in inputs.items()}
    tok, att, ffn = ({n[len(k):]: x for n, x in i.items() if n.startswith(k)} for k in ("L0_tok_", "L0_attn_", "L0_ffn_"))

    def padded(rows, *parts):
        parts = [p.reshape(-1, p.shape[-1]) for p in parts]
        return np.concatenate(parts + [np.zeros((rows - sum(len(p) for p in parts), parts[0].shape[1]), f)], 0)

    wva = np.zeros((D + 1, H, VW), f)
    wva[:D, :, :DK] = att["v_w"].T.reshape(D, H, DK)
    wva[D, :, :DK] = att["v_b"].reshape(H, DK)
    wva[D, :, DK] = 1.0
    taps = att["conv_w"].transpose(2, 1, 0)
    cw = np.zeros((P, 3, D), f)
    for k in range(TAPS):
        cw[D * (k % 2):D * (k % 2) + D, k // 2] = taps[k]
    r, x = np.arange(P)[:, None], np.arange(T)[None, :]
    arrays = {
        "xT": i["x"].reshape(B, T, D).transpose(0, 2, 1),
        "gammaT": tok["d_gamma_batched"].T.reshape(NB, P, T).transpose(1, 0, 2),
        "wq": padded(KP, tok["Wq"], tok["bq"]), "wk": padded(KP, tok["Wk"], tok["bk"]), "wv": padded(KP, tok["Wv"], tok["bv"]),
        "wo2": np.concatenate([tok["Wo"], tok["Wo"]], 0),
        "bo_row": padded(KP, np.tile(tok["bo"], NB)),
        "cb_row": padded(KP, np.tile(att["conv_b"], NB)),
        "beta": np.repeat(att["sqrt_beta"].reshape(1, D), P, 0),
        "conv_w": cw,
        "prelu": np.repeat(tok["prelu_a"].reshape(1, 1), P, 0),
        "ln_wb": np.stack([att["ln_w"], att["ln_b"]], 1),
        "wqk": padded(KP, np.concatenate([att["q_w"].T, att["k_w"].T], 1), np.concatenate([att["q_b"], att["k_b"]])),
        "wva": padded(KP, wva.reshape(D + 1, H * VW)),
        "gammas": np.repeat(att["gammas"].reshape(1, H), P, 0),
        "ow": padded(KP, att["out_w"].T, att["out_b"]),
        "rw": padded(KP, ffn["router_w"].T, ffn["router_b"]),
        "w1": padded(KP, ffn["W1"].transpose(1, 0, 2).reshape(D, E * HID), ffn["b1"].reshape(1, E * HID)),
        "w2": ffn["W2"].reshape(E * HID // P, P, D).transpose(1, 0, 2),
        "b2": padded(KP, ffn["b2"]),
        "c_ident": np.eye(P, dtype=f),
        "c_mask": np.where(np.arange(P)[None, :] > r, f(MASKED), f(0)).astype(f),
        "c_pos": np.maximum(r + T - P - x, 0).astype(f),
        "c_ones_row": padded(KP, np.ones((1, P), f)),
        "c_eps12": np.full((P, 1), 1e-12, f), "c_eps5": np.full((P, 1), 1e-5, f),
        "c_qk_scale": np.concatenate([np.full((D, 1), DK ** -0.5, f), np.ones((D, 1), f)], 0),
        "c_expand": padded(KP, np.repeat(np.eye(E, dtype=f), HID, 1) * f(1e30)),
        "c_prio": np.repeat(np.arange(E, 0, -1, dtype=f)[None], P, 0),
        "c_rowmask": (r > 0).astype(f),
    }
    nc = bacc.Bacc("TRN2", target_bir_lowering=False, num_devices=1)
    arrays = {n: np.ascontiguousarray(x) for n, x in arrays.items()}
    a = {n: nc.dram_tensor("in_" + n, x.shape, mybir.dt.from_np(x.dtype), kind="ExternalInput").ap() for n, x in arrays.items()}
    out = nc.dram_tensor("out_rows", (B, T, D), F32, kind="ExternalOutput").ap()
    program(nc, a, out)
    got = run_bass_kernel_spmd(nc, [{"in_" + n: x for n, x in arrays.items()}], core_ids=[0])
    return got.results[0]["out_rows"]
```
